# Optimizing a Trainium2 kernel written in Bass

```python
import numpy as np
import jax
import jax.numpy as jnp

def _softmax(x, axis=-1):
    return jax.nn.softmax(x, axis=axis)

def _gelu(x):
    return jax.nn.gelu(x, approximate=True)

def _silu(x):
    return jax.nn.silu(x)

def _sigmoid(x):
    return jax.nn.sigmoid(x)

def _layernorm(x, axis=-1, eps=1e-05):
    m = jnp.mean(x, axis=axis, keepdims=True)
    v = jnp.var(x, axis=axis, keepdims=True)
    return (x - m) / jnp.sqrt(v + eps)

def _scatter_add(tgt, idx, src, axis=0):
    return tgt.at[idx].add(src)

def _segment_sum(src, seg, n):
    return jax.ops.segment_sum(src, seg, n)
kernel_name = 'mk_flamingo_gated_d1_seqx_r8_686d32'

def setup_inputs(seed: int=0):
    np.random.seed(seed)
    _w = jnp.asarray

    def _rec_inputs():
        import jax
        import jax.numpy as jnp
        _rk = jax.random.key(seed)
        x = -0.0003929 + 0.9999 * jax.random.normal(jax.random.fold_in(_rk, 1), (16, 56, 256), jnp.float32)
        _lenS = 56 - jax.random.randint(jax.random.fold_in(_rk, 7), (16,), 0, max(1, 56 // 4) + 1, jnp.int32)
        _lenS2 = 1500 - jax.random.randint(jax.random.fold_in(_rk, 8), (16,), 0, max(1, 1500 // 4) + 1, jnp.int32)
        _ctx_2048P = jax.random.normal(jax.random.fold_in(_rk, 11), (16, 16, 256), jnp.float32)
        _ctx_2048c = jax.random.dirichlet(jax.random.fold_in(_rk, 511), 0.3 * jnp.ones((16,), jnp.float32), (16, 1500))
        _ctx_2048t = jnp.einsum('bsk,bkd->bsd', _ctx_2048c, _ctx_2048P)
        _ctx_2048t = _ctx_2048t * jax.lax.rsqrt(jnp.mean(jnp.square(_ctx_2048t)) + 1e-12) * 0.953939
        ctx_2048 = -0.000514642 + 1.00011 * (_ctx_2048t + 0.3 * jax.random.normal(jax.random.fold_in(_rk, 611), (16, 1500, 256), jnp.float32))
        _validS = jnp.arange(56)[None, :] < _lenS[:, None]
        _validS2 = jnp.arange(1500)[None, :] < _lenS2[:, None]
        _causal = jnp.tril(jnp.ones((56, 56), dtype=bool))
        mask_BxS2_ik0 = jnp.where(jnp.broadcast_to(_validS2[:, :], (16, 1500)), 0, 1).astype(jnp.int32)
        _g = jax.random.normal(jax.random.fold_in(_rk, 9001), (2, 1), jnp.float32)
        _g = jnp.sign(_g) * jnp.maximum(jnp.abs(_g), 1.0) + (_g == 0) * 1.0
        g_xattn = _g[0]
        g_ffn = _g[1]
        return (x, ctx_2048, mask_BxS2_ik0, g_xattn, g_ffn)
    x, ctx_2048, mask_BxS2_ik0, g_xattn, g_ffn = _rec_inputs()

    def _L0_xattn_setup():
        import jax, jax.numpy as jnp
        import numpy as np
        import math
        H = 256
        NH = 16
        HD = H // NH
        EPS_LN = 1e-05
        RES_SCALE_MAX = 0.3

        def _nan_clean(x, lim=10000.0):
            return jnp.nan_to_num(x, nan=0.0, posinf=lim, neginf=-lim)
        key = jax.random.key(seed)
        ks = jax.random.split(key, 12)
        B, S, T = (4, 256, 32)
        std = 1.0 / math.sqrt(H)
        return {'hidden_states': jax.random.normal(ks[0], (B, S, H), jnp.float32), 'audio_tokens': jax.random.normal(ks[1], (B, T, H), jnp.float32), 'attention_mask': jax.random.randint(ks[2], (B, T), 0, 2, jnp.int32), 'Wq': jax.random.normal(ks[3], (H, H), jnp.float32) * std, 'bq': jnp.zeros((H,), jnp.float32), 'Wk': jax.random.normal(ks[4], (H, H), jnp.float32) * std, 'bk': jnp.zeros((H,), jnp.float32), 'Wv': jax.random.normal(ks[5], (H, H), jnp.float32) * std, 'bv': jnp.zeros((H,), jnp.float32), 'Wo': jax.random.normal(ks[6], (H, H), jnp.float32) * std, 'bo': jnp.zeros((H,), jnp.float32), 'ln_gamma': jnp.ones((H,), jnp.float32), 'ln_beta': jnp.zeros((H,), jnp.float32), 'residual_scale': jnp.float32(0.05)}
    _L0_xattn_all = _L0_xattn_setup()
    _L0_xattn_in = {k: v for k, v in _L0_xattn_all.items() if k in ('Wq', 'bq', 'Wk', 'bk', 'Wv', 'bv', 'Wo', 'bo', 'ln_gamma', 'ln_beta', 'residual_scale')}
    del _L0_xattn_all

    def _L0_ffn_setup():
        import jax, jax.numpy as jnp
        import numpy as np
        NUM_EXPERTS = 8
        TOP_K = 2
        MODEL_DIM = 256
        INTER_DIM = 128
        GATE_SCALE = 1.0
        UP_SCALE = 0.0
        key = jax.random.key(seed)
        k1, k2, k3, k4 = jax.random.split(key, 4)
        hidden_states = jax.random.normal(k1, (2, 256, MODEL_DIM), jnp.float32)
        router_gate = jax.random.normal(k2, (NUM_EXPERTS, MODEL_DIM), jnp.float32) * 0.02
        expert_gate_up = jax.random.normal(k3, (NUM_EXPERTS, MODEL_DIM, 2 * INTER_DIM), jnp.float32) * 0.02
        expert_down = jax.random.normal(k4, (NUM_EXPERTS, INTER_DIM, MODEL_DIM), jnp.float32) * 0.02
        return {'hidden_states': hidden_states, 'router_gate': router_gate, 'expert_gate_up': expert_gate_up, 'expert_down': expert_down}
    _L0_ffn_all = _L0_ffn_setup()
    _L0_ffn_in = {k: v for k, v in _L0_ffn_all.items() if k in ('router_gate', 'expert_gate_up', 'expert_down')}
    del _L0_ffn_all
    return {'x': x, 'ctx_2048': ctx_2048, 'mask_BxS2_ik0': mask_BxS2_ik0, 'g_xattn': g_xattn, 'g_ffn': g_ffn, 'L0_xattn_Wq': _L0_xattn_in['Wq'], 'L0_xattn_bq': _L0_xattn_in['bq'], 'L0_xattn_Wk': _L0_xattn_in['Wk'], 'L0_xattn_bk': _L0_xattn_in['bk'], 'L0_xattn_Wv': _L0_xattn_in['Wv'], 'L0_xattn_bv': _L0_xattn_in['bv'], 'L0_xattn_Wo': _L0_xattn_in['Wo'], 'L0_xattn_bo': _L0_xattn_in['bo'], 'L0_xattn_ln_gamma': _L0_xattn_in['ln_gamma'], 'L0_xattn_ln_beta': _L0_xattn_in['ln_beta'], 'L0_xattn_residual_scale': _L0_xattn_in['residual_scale'], 'L0_ffn_router_gate': _L0_ffn_in['router_gate'], 'L0_ffn_expert_gate_up': _L0_ffn_in['expert_gate_up'], 'L0_ffn_expert_down': _L0_ffn_in['expert_down']}

def reference(x, ctx_2048, mask_BxS2_ik0, g_xattn, g_ffn, L0_xattn_Wq, L0_xattn_bq, L0_xattn_Wk, L0_xattn_bk, L0_xattn_Wv, L0_xattn_bv, L0_xattn_Wo, L0_xattn_bo, L0_xattn_ln_gamma, L0_xattn_ln_beta, L0_xattn_residual_scale, L0_ffn_router_gate, L0_ffn_expert_gate_up, L0_ffn_expert_down):
    import jax
    import jax.numpy as jnp

    def _L0_xattn_ref(hidden_states, audio_tokens, attention_mask, Wq, bq, Wk, bk, Wv, bv, Wo, bo, ln_gamma, ln_beta, residual_scale):
        import jax, jax.numpy as jnp
        import numpy as np
        import math
        H = 256
        NH = 16
        HD = H // NH
        EPS_LN = 1e-05
        RES_SCALE_MAX = 0.3

        def _nan_clean(x, lim=10000.0):
            return jnp.nan_to_num(x, nan=0.0, posinf=lim, neginf=-lim)
        B, S, _ = hidden_states.shape
        T = audio_tokens.shape[1]
        hs = _nan_clean(hidden_states).astype(jnp.float32)
        at = _nan_clean(audio_tokens).astype(jnp.float32)

        def proj(x, W, b, L):
            y = x @ W.T + b
            return y.reshape(B, L, NH, HD).transpose(0, 2, 1, 3)
        q = _nan_clean(proj(hs, Wq, bq, S))
        k = _nan_clean(proj(at, Wk, bk, T))
        v = _nan_clean(proj(at, Wv, bv, T))
        scale = max(math.sqrt(HD), 1e-08)
        scores = jnp.einsum('bhsd,bhtd->bhst', q, k) / scale
        scores = jnp.clip(scores, -50.0, 50.0)
        scores = jnp.nan_to_num(scores, nan=0.0, posinf=50.0, neginf=-50.0)
        attend = (attention_mask.astype(jnp.float32) > 0.5)[:, None, None, :]
        scores = jnp.where(attend, scores, -10000.0)
        scores = jnp.clip(scores, -50.0, 50.0)
        probs = jax.nn.softmax(scores, axis=-1)
        probs = jnp.nan_to_num(probs, nan=0.0, posinf=1.0, neginf=0.0)
        probs = probs / (probs.sum(axis=-1, keepdims=True) + 1e-08)
        ctx = jnp.einsum('bhst,bhtd->bhsd', probs, v)
        ctx = ctx.transpose(0, 2, 1, 3).reshape(B, S, H)
        delta = _nan_clean(ctx @ Wo.T + bo)
        rs = jnp.clip(residual_scale, 0.0, RES_SCALE_MAX)
        delta = rs * delta
        mu = delta.mean(axis=-1, keepdims=True)
        var = jnp.mean((delta - mu) ** 2, axis=-1, keepdims=True)
        delta = (delta - mu) / jnp.sqrt(var + EPS_LN) * ln_gamma + ln_beta
        return delta

    def _L0_ffn_ref(hidden_states, router_gate, expert_gate_up, expert_down):
        import jax, jax.numpy as jnp
        import numpy as np
        NUM_EXPERTS = 8
        TOP_K = 2
        MODEL_DIM = 256
        INTER_DIM = 128
        GATE_SCALE = 1.0
        UP_SCALE = 0.0
        orig_shape = hidden_states.shape
        hs = hidden_states.reshape(-1, orig_shape[-1])
        T = hs.shape[0]
        logits = hs @ router_gate.T
        probs = jax.nn.softmax(logits.astype(jnp.float32), axis=-1)
        topk_scores, topk_idx = jax.lax.top_k(probs, TOP_K)
        topk_scores = topk_scores / jnp.sum(topk_scores, axis=-1, keepdims=True)
        scores_f = topk_scores.T.reshape(-1).astype(hs.dtype)
        ids_f = topk_idx.T.reshape(-1)
        order = jnp.argsort(ids_f)
        sorted_ids = ids_f[order]
        scores_sorted = scores_f[order]
        token_slots = order % T
        x = hs[token_slots]
        inter = jnp.zeros((x.shape[0], 2 * INTER_DIM), x.dtype)
        for e in range(NUM_EXPERTS):
            m = (sorted_ids == e)[:, None]
            inter = inter + jnp.where(m, x, 0) @ expert_gate_up[e]
        gate = inter[..., 0::2]
        up = inter[..., 1::2]
        h = (up + UP_SCALE) * jax.nn.silu(gate * GATE_SCALE)
        out_rows = jnp.zeros((x.shape[0], MODEL_DIM), x.dtype)
        for e in range(NUM_EXPERTS):
            m = (sorted_ids == e)[:, None]
            out_rows = out_rows + jnp.where(m, h, 0) @ expert_down[e]
        out = jnp.zeros_like(hs).at[token_slots].add(out_rows * scores_sorted[:, None])
        return out.reshape(orig_shape)
    x = x + jnp.tanh(g_xattn[0]) * _L0_xattn_ref(_layernorm(x, axis=-1), ctx_2048, mask_BxS2_ik0, L0_xattn_Wq, L0_xattn_bq, L0_xattn_Wk, L0_xattn_bk, L0_xattn_Wv, L0_xattn_bv, L0_xattn_Wo, L0_xattn_bo, L0_xattn_ln_gamma, L0_xattn_ln_beta, L0_xattn_residual_scale)
    x = x + jnp.tanh(g_ffn[0]) * _L0_ffn_ref(_layernorm(x, axis=-1), L0_ffn_router_gate, L0_ffn_expert_gate_up, L0_ffn_expert_down)
    return x

_drawn_inputs = setup_inputs


def setup_inputs(seed=0):
    import zlib

    import numpy as np

    out = dict(_drawn_inputs(seed))
    spreads = {'L0_xattn_bq': (0.0, 0.308),
     'L0_xattn_bk': (0.0, 0.8),
     'L0_xattn_bv': (0.0, 0.1),
     'L0_xattn_bo': (0.0, 0.1),
     'L0_xattn_ln_gamma': (1.0, 0.2),
     'L0_xattn_ln_beta': (0.0, 0.1)}
    factors = {'L0_ffn_router_gate': 8.0, 'L0_ffn_expert_gate_up': 8.0, 'L0_ffn_expert_down': 8.0}
    for name, (base, spread) in spreads.items():
        noise = np.random.default_rng([zlib.crc32(name.encode()), seed]).standard_normal(out[name].shape)
        drawn = base * np.exp(spread * noise) if base else spread * noise
        out[name] = jnp.asarray(drawn.astype(out[name].dtype))
    for name, factor in factors.items():
        out[name] = (out[name] * factor).astype(out[name].dtype)
    return out
```

```python
from contextlib import ExitStack

import numpy as np

import concourse.bass as bass
from concourse import mybir

F32 = mybir.dt.float32
I32 = mybir.dt.int32
ALU = mybir.AluOpType
ACT = mybir.ActivationFunctionType
AX_X = mybir.AxisListType.X

P = 128
B, S, H = 16, 56, 256
T = 1500
NH, HD = 16, 16
HALVES = H // P
CHUNKS = 3
CT = T // CHUNKS
TT = 125
TPC = CT // TT
NT = T // TT
HH = NH // HALVES
HALF = HH * S
ROWS = B * S
RT = ROWS // P
NV, NP_ = 4, 3
GROUPS = 4
SLOTS = NH // GROUPS
ACC = SLOTS * S
NE, FF = 8, 128
EPS_LN = 1e-5
CLIP = 50.0
E_HI, E_LO = float(np.exp(50.0)), float(np.exp(-50.0))
FMAX = float(np.finfo(np.float32).max)
LIM = 10000.0


def flamingo(nc, x_d, ctx_d, mask_d, gx_d, gf_d, wq_d, bq_d, wk_d, bk_d, wv_d, bv_d, wo_d, bo_d,
             gamma_d, beta_d, rs_d, router_d, gate_up_d, down_d, out_d):
    with ExitStack() as ctx:
        def sb(name, shape, dt=F32):
            return ctx.enter_context(nc.sbuf_tensor(name, shape, dt))

        def sem(name):
            return ctx.enter_context(nc.semaphore(name))

        def after(engine, semaphore, count):
            if isinstance(count, int) and count <= 0:
                return
            engine.wait_ge(semaphore, count)

        ident = sb("ident", [P, P])
        head_mask = sb("head_mask", [P, HH])
        den_select = sb("den_select", [P, P])
        later_expert = sb("later_expert", [P, NE, NE])
        wq, wk, wv = (sb(n, [P, HALVES, H]) for n in ("wq", "wk", "wv"))
        wo = sb("wo", [P, SLOTS, H])
        bq, bk = sb("bq", [P, HALVES]), sb("bk", [P, HALVES])
        bv, bo, gamma, beta = (sb(n, [P, H]) for n in ("bv", "bo", "gamma", "beta"))
        router = sb("router", [P, HALVES, NE])
        gate_up = sb("gate_up", [P, NE, HALVES, 2, FF])
        down = sb("down", [P, NE, H])
        gates = sb("gates", [P, 3])
        tanhs = sb("tanhs", [P, 2])
        rscale = sb("rscale", [P, 1])
        mask_i = sb("mask_i", [P, B * NT], I32)
        attend = sb("attend", [P, B * NT])
        mask_scale = sb("mask_scale", [P, NT])
        mask_bias = sb("mask_bias", [P, NT])
        x_sb = sb("x_sb", [P, RT, H])
        normed = sb("normed", [P, RT, H])
        fix = sb("fix", [P, RT * H])
        fix_neg = sb("fix_neg", [P, RT * H])
        finite = sb("finite", [P, RT * H], I32)
        stats = sb("stats", [P, RT, 6])
        moments = sb("moments", [P, RT, 2])
        var_eps, rstd, newton = sb("var_eps", [P, RT]), sb("rstd", [P, RT]), sb("newton", [P, RT])
        rowsT = sb("rowsT", [P, HALVES, ROWS])
        qT = sb("qT", [P, HALVES, ROWS])
        ctxT = [sb(f"ctxT{c}", [P, HALVES, CT]) for c in range(CHUNKS)]
        kT = [sb(f"kT{c}", [P, HALVES, CT]) for c in range(CHUNKS)]
        qbd = sb("qbd", [P, HALVES, HH, S])
        v = [sb(f"v{n}", [TT, NH, 2 * HD]) for n in range(NV)]
        p = [sb(f"p{n}", [TT, NH * S]) for n in range(NP_)]
        acc_sb, den_sb, inv_den = (sb(n, [P, ACC]) for n in ("acc_sb", "den_sb", "inv_den"))
        ctxn = sb("ctxn", [P, SLOTS, ROWS])
        logits = sb("logits", [P, RT, NE])
        probs = sb("probs", [P, RT, NE])
        weight = sb("weight", [P, RT, NE])
        above, ties = sb("above", [P, RT, NE, NE]), sb("ties", [P, RT, NE, NE])
        row_max, row_sum, row_inv = sb("row_max", [P, RT]), sb("row_sum", [P, RT]), sb("row_inv", [P, RT])
        silu = sb("silu", [P, 2, HALF])
        act = sb("act", [P, 2, ROWS])
        y = sb("y", [P, RT, H])

        bank = ctx.enter_context(nc.psum_tensor("bank", [P, 8, 512], F32))
        S_BANK = [0, 2]
        K_BANK = 4
        V_BANK = 6
        ACC_BANK = 7
        acc = bank[:, ACC_BANK, 0:ACC]
        den = bank[:, ACC_BANK, 256:256 + ACC]

        x_in, small_in, qk_in, v_in, late_in = (sem(n) for n in ("x_in", "small_in", "qk_in", "v_in", "late_in"))
        ctx_in = [sem(f"ctx_in{c}") for c in range(CHUNKS)]
        consts = sem("consts")
        chain = sem("chain")
        var_ready, std_ready = sem("var_ready"), sem("std_ready")
        tanh_ready, wo_clear = sem("tanh_ready"), sem("wo_clear")
        rows_ready = sem("rows_ready")
        t_mm, t_out = sem("t_mm"), sem("t_out")
        q_mm, q_out, q_clean = sem("q_mm"), sem("q_out"), sem("q_clean")
        mask_ready, v_ones = sem("mask_ready"), sem("v_ones")
        qbd_clear, qbd_ready = sem("qbd_clear"), sem("qbd_ready")
        k_mm, k_out = sem("k_mm"), sem("k_out")
        v_mm, v_out = sem("v_mm"), sem("v_out")
        s_mm, exp_out, p_out = sem("s_mm"), sem("exp_out"), sem("p_out")
        pv_mm, acc_out, den_mm, den_out = sem("pv_mm"), sem("acc_out"), sem("den_mm"), sem("den_out")
        epi = sem("epi")
        o_mm, o_out = sem("o_mm"), sem("o_out")
        r_mm, r_out, e_out = sem("r_mm"), sem("r_out"), sem("e_out")
        shifted = sem("shifted")
        gu_mm, silu_out, act_out = sem("gu_mm"), sem("silu_out"), sem("act_out")
        d_mm, d_out = sem("d_mm"), sem("d_out")
        y_done, stored = sem("y_done"), sem("stored")

        block = ctx.enter_context(nc.Block())

        @block.sync
        def _(sp):
            sp.dma_start(x_sb[:], x_d.rearrange("(r p) h -> p r h", p=P)).then_inc(x_in, 16)
            sp.dma_start(wk[:], wk_d).then_inc(qk_in, 16)
            sp.dma_start(ctxT[0][:], ctx_d[0, 0]).then_inc(ctx_in[0], 16)
            sp.dma_start(wq[:], wq_d).then_inc(qk_in, 16)
            sp.dma_start(wv[:], wv_d).then_inc(v_in, 16)
            sp.dma_start(bv[:], bv_d.partition_broadcast(P)).then_inc(v_in, 16)
            for c in range(1, CHUNKS):
                sp.dma_start(ctxT[c][:], ctx_d[0, c]).then_inc(ctx_in[c], 16)
            sp.wait_ge(wo_clear, 1)
            for j in range(GROUPS):
                sp.dma_start(wo[2 * HD * j:2 * HD * j + HD], wo_d[j]).then_inc(late_in, 16)
            for tile, source in ((bo, bo_d), (gamma, gamma_d), (beta, beta_d)):
                sp.dma_start(tile[:], source.partition_broadcast(P)).then_inc(late_in, 16)
            for tile, source in ((router, router_d), (gate_up, gate_up_d), (down, down_d)):
                sp.dma_start(tile[:], source).then_inc(late_in, 16)

            with sp.Fori(1, B) as b:
                for c in range(CHUNKS):
                    sp.wait_ge(v_mm, (b - 1) * NT + TPC * (c + 1))
                    sp.dma_start(ctxT[c][:], ctx_d[b, c]).then_inc(ctx_in[c], 16)
            sp.wait_ge(y_done, 1)
            sp.dma_start(out_d.rearrange("(r p) h -> p r h", p=P), normed[:]).then_inc(stored, 16)
            sp.wait_ge(stored, 16)
        LATE = 16 * (GROUPS + 6)

        @block.gpsimd
        def _(pool):
            for tile, source in ((bq, bq_d), (bk, bk_d)):
                pool.dma_start(tile[:], source).then_inc(small_in, 16)
            pool.dma_start(mask_i[0:TT], mask_d).then_inc(small_in, 16)
            for n, source in enumerate((gx_d, gf_d, rs_d)):
                pool.dma_start(gates[:, n:n + 1], source.partition_broadcast(P)).then_inc(small_in, 16)
            nc.gpsimd.memset(ident[:], 0.0).then_inc(consts, 1)
            nc.gpsimd.memset(head_mask[:], 1.0).then_inc(consts, 1)
            nc.gpsimd.memset(den_select[:], 0.0).then_inc(consts, 1)
            nc.gpsimd.memset(later_expert[:], 1.0).then_inc(consts, 1)
            nc.gpsimd.memset(wo[:], 0.0).then_inc(wo_clear, 1)
            pool.wait_ge(consts, 4)
            nc.gpsimd.affine_select(out=ident[:], in_=ident[:], compare_op=ALU.not_equal, fill=1.0, base=0,
                                    pattern=[[-1, P]], channel_multiplier=1).then_inc(consts, 1)
            nc.gpsimd.affine_select(out=head_mask[:], in_=head_mask[:], compare_op=ALU.is_ge, fill=0.0, base=0,
                                    pattern=[[-HD, HH]], channel_multiplier=1).then_inc(consts, 1)
            pool.wait_ge(consts, 6)
            nc.gpsimd.affine_select(out=head_mask[:], in_=head_mask[:], compare_op=ALU.is_ge, fill=0.0, base=HD - 1,
                                    pattern=[[HD, HH]], channel_multiplier=-1).then_inc(consts, 1)
            sel = den_select[:].rearrange("k (j m) -> k j m", j=GROUPS)
            nc.gpsimd.affine_select(out=sel, in_=sel, compare_op=ALU.not_equal, fill=1.0, base=-HD,
                                    pattern=[[-2 * HD, GROUPS], [0, 2 * HD]], channel_multiplier=1).then_inc(consts, 1)
            nc.gpsimd.affine_select(out=later_expert[:], in_=later_expert[:], compare_op=ALU.is_ge, fill=0.0,
                                    base=-1, pattern=[[1, NE], [-1, NE]], channel_multiplier=0).then_inc(consts, 1)
        CONSTS = 9
        SMALL = 16 * 6

        @block.tensor
        def _(pe):
            def transposes(first):
                for r in range(RT):
                    pe.wait_ge(rows_ready, first + r + 1)
                    if first + r >= 2:
                        pe.wait_ge(t_out, first + r - 1)
                    for k in range(HALVES):
                        mm = nc.tensor.transpose(bank[:, (first + r) % 2, P * k:P * (k + 1)],
                                                 normed[:, r, P * k:P * (k + 1)], ident[:])
                    mm.then_inc(t_mm, 1)

            def k_proj(b, c, m):
                if m == 0:
                    pe.wait_ge(ctx_in[c], 16 * b + 16)
                after(pe, k_out, HALVES * (CHUNKS * b + c - 1) + m + 1)
                for k in range(HALVES):
                    mm = nc.tensor.matmul(bank[:, K_BANK + m, 0:CT], wk[:, k, P * m:P * (m + 1)],
                                          ctxT[c][:, k, :], start=(k == 0), stop=(k == HALVES - 1))
                mm.then_inc(k_mm, 1)

            def v_proj(b, i):
                c, t0 = i // TPC, TT * (i % TPC)
                after(pe, v_out, NT * b + i)
                for k in range(HALVES):
                    mm = nc.tensor.matmul(bank[0:TT, V_BANK, 0:H], ctxT[c][:, k, t0:t0 + TT], wv[:, k, :],
                                          start=(k == 0), stop=(k == HALVES - 1))
                mm.then_inc(v_mm, 1)

            def scores(b, i):
                c, t0 = i // TPC, TT * (i % TPC)
                if i == 0:
                    pe.wait_ge(qbd_ready, b + 1)
                for m in range(HALVES):
                    if i % TPC == 0:
                        pe.wait_ge(k_out, HALVES * (CHUNKS * b + c) + m + 1)
                    after(pe, exp_out, HALVES * (NT * b + i - 2) + m + 1)
                    nc.tensor.matmul(bank[0:TT, S_BANK[i % 2] + m, 0:HALF], kT[c][:, m, t0:t0 + TT],
                                     qbd[:, m], start=True, stop=True).then_inc(s_mm, 1)

            def p_v(b, i):
                pe.wait_ge(v_out, NT * b + i + 1)
                if i == 0:
                    after(pe, den_out, b)
                for slot in range(SLOTS):
                    for j in range(GROUPS):
                        h = GROUPS * slot + j
                        if h % HH == 0:
                            pe.wait_ge(p_out, HALVES * (NT * b + i) + h // HH + 1)
                        mm = nc.tensor.matmul(acc[2 * HD * j:2 * HD * (j + 1), S * slot:S * (slot + 1)],
                                              v[i % NV][:, h, :], p[i % NP_][:, S * h:S * (h + 1)],
                                              start=(i == 0 and slot == 0), stop=(i == NT - 1),
                                              skip_group_check=True)
                mm.then_inc(pv_mm, 1)

            def denominators(b):
                pe.wait_ge(acc_out, b + 1)
                nc.tensor.matmul(den, den_select[:], acc_sb[:], start=True, stop=True,
                                 skip_group_check=True).then_inc(den_mm, 1)

            def batch(b, first, last):
                for i in range(NT):
                    scores(b, i)
                    v_proj(b, i)
                    if i == 0 and not first:
                        denominators(b - 1)
                    c = i // TPC
                    if i % TPC in (1, 2) and c + 1 < CHUNKS:
                        k_proj(b, c + 1, i % TPC - 1)
                    if i > 0:
                        p_v(b, i - 1)
                if not last:
                    for m in range(HALVES):
                        k_proj(b + 1, 0, m)
                p_v(b, NT - 1)

            pe.wait_ge(consts, CONSTS)
            pe.wait_ge(qk_in, 32)
            k_proj(0, 0, 0)
            k_proj(0, 0, 1)
            transposes(0)
            pe.wait_ge(t_out, RT)
            for n in range(2):
                for m in range(HALVES):
                    if n:
                        pe.wait_ge(q_out, m + 1)
                    for k in range(HALVES):
                        mm = nc.tensor.matmul(bank[:, 2 + m, 0:HALF], wq[:, k, P * m:P * (m + 1)],
                                              rowsT[:, k, HALF * n:HALF * (n + 1)],
                                              start=(k == 0), stop=(k == HALVES - 1))
                    mm.then_inc(q_mm, 1)
            pe.wait_ge(q_out, 4)
            pe.wait_ge(v_in, 32)
            pe.wait_ge(v_ones, NV)
            batch(0, True, False)
            with pe.Fori(1, B - 1) as b:
                batch(b, False, False)
            batch(B - 1, False, True)
            denominators(B - 1)

            pe.wait_ge(late_in, LATE)
            pe.wait_ge(epi, 3 * B)
            for r in range(RT):
                if r >= 2:
                    pe.wait_ge(o_out, r - 1)
                for slot in range(SLOTS):
                    mm = nc.tensor.matmul(bank[:, r % 2, 0:H], ctxn[:, slot, P * r:P * (r + 1)], wo[:, slot, :],
                                          start=(slot == 0), stop=(slot == SLOTS - 1))
                mm.then_inc(o_mm, 1)
            transposes(RT)
            pe.wait_ge(t_out, 2 * RT)
            for r in range(RT):
                for k in range(HALVES):
                    mm = nc.tensor.matmul(bank[:, 2, NE * r:NE * (r + 1)], rowsT[:, k, P * r:P * (r + 1)],
                                          router[:, k, :], start=(k == 0), stop=(k == HALVES - 1))
            mm.then_inc(r_mm, 1)

            def expert_in(e):
                for n in range(2):
                    step = 2 * e + n
                    if step >= 2:
                        pe.wait_ge(act_out, step - 1)
                    for g in range(2):
                        for k in range(HALVES):
                            mm = nc.tensor.matmul(bank[:, 4 + 2 * n + g, 0:HALF], gate_up[:, e, k, g, :],
                                                  rowsT[:, k, HALF * n:HALF * (n + 1)],
                                                  start=(k == 0), stop=(k == HALVES - 1))
                    mm.then_inc(gu_mm, 1)

            def expert_out(e):
                for r in range(RT):
                    step = RT * e + r
                    if r == 0:
                        pe.wait_ge(act_out, 2 * e + 1)
                    if r == RT // 2:
                        pe.wait_ge(act_out, 2 * e + 2)
                    if step >= 2:
                        pe.wait_ge(d_out, step - 1)
                    nc.tensor.matmul(bank[:, step % 2, 0:H], act[:, e % 2, P * r:P * (r + 1)], down[:, e, :],
                                     start=True, stop=True).then_inc(d_mm, 1)

            expert_in(0)
            for e in range(NE):
                if e + 1 < NE:
                    expert_in(e + 1)
                expert_out(e)

        @block.scalar
        def _(act_e):
            def sqrt_var(n):
                act_e.wait_ge(var_ready, n + 1)
                nc.scalar.activation(rstd[:], var_eps[:], ACT.Sqrt).then_inc(std_ready, 1)

            def k_copy(b, c, m):
                act_e.wait_ge(k_mm, HALVES * (CHUNKS * b + c) + m + 1)
                after(act_e, s_mm, HALVES * (NT * (b - 1) + TPC * (c + 1)))
                nc.scalar.activation(kT[c][:, m, :], bank[:, K_BANK + m, 0:CT], ACT.Identity,
                                     bias=bk[:, m:m + 1]).then_inc(k_out, 1)

            def exps(b, i):
                after(act_e, pv_mm, NT * b + i - NP_ + 1)
                if i == 0:
                    act_e.wait_ge(mask_ready, b + 1)
                for m in range(HALVES):
                    act_e.wait_ge(s_mm, HALVES * (NT * b + i) + m + 1)
                    nc.scalar.activation(p[i % NP_][:, HALF * m:HALF * (m + 1)],
                                         bank[0:TT, S_BANK[i % 2] + m, 0:HALF], ACT.Exp,
                                         bias=mask_bias[0:TT, i:i + 1],
                                         scale=mask_scale[0:TT, i:i + 1]).then_inc(exp_out, 1)

            def batch(b, last):
                for i in range(NT):
                    exps(b, i)
                    c = i // TPC
                    if i % TPC in (1, 2) and c + 1 < CHUNKS:
                        k_copy(b, c + 1, i % TPC - 1)
                if not last:
                    for m in range(HALVES):
                        k_copy(b + 1, 0, m)

            act_e.wait_ge(small_in, SMALL)
            sqrt_var(0)
            k_copy(0, 0, 0)
            k_copy(0, 0, 1)
            nc.scalar.activation(tanhs[:], gates[:, 0:2], ACT.Tanh).then_inc(tanh_ready, 1)
            for n in range(2):
                for m in range(HALVES):
                    act_e.wait_ge(q_mm, 2 * n + m + 1)
                    nc.scalar.activation(qT[:, m, HALF * n:HALF * (n + 1)], bank[:, 2 + m, 0:HALF], ACT.Identity,
                                         bias=bq[:, m:m + 1]).then_inc(q_out, 1)
            batch(0, False)
            with act_e.Fori(1, B - 1) as b:
                batch(b, False)
            batch(B - 1, True)

            sqrt_var(1)
            sqrt_var(2)
            act_e.wait_ge(shifted, 1)
            nc.scalar.activation(probs[:], logits[:], ACT.Exp).then_inc(e_out, 1)
            for step in range(2 * NE):
                act_e.wait_ge(gu_mm, step + 1)
                if step >= 2:
                    act_e.wait_ge(act_out, step - 1)
                nc.scalar.activation(silu[:, step % 2, :], bank[:, 4 + 2 * (step % 2), 0:HALF],
                                     ACT.Silu).then_inc(silu_out, 1)

        @block.vector
        def _(dve):
            count = [0]

            def step(ins):
                count[0] += 1
                ins.then_inc(chain, 1)
                dve.wait_ge(chain, count[0])

            def clean(t, n):
                f, g, m = fix[:, 0:n], fix_neg[:, 0:n], finite[:, 0:n]
                step(nc.vector.tensor_scalar(f, t, 0.0, LIM, ALU.max, ALU.min))
                step(nc.vector.tensor_scalar(g, t, 0.0, -LIM, ALU.min, ALU.max))
                step(nc.vector.tensor_scalar(m, t, 0.0, 0.0, ALU.mult, ALU.is_equal))
                step(nc.vector.tensor_tensor(f, f, g, ALU.add))
                step(nc.vector.copy_predicated(f, m, t))

            def layernorm(src, dst, n):
                for r in range(RT):
                    step(nc.vector.bn_stats(stats[:, r, :], src[:, r, :]))
                for r in range(RT):
                    step(nc.vector.bn_aggr(moments[:, r, :], stats[:, r, :]))
                step(nc.vector.tensor_scalar(var_eps[:], moments[:, :, 1], EPS_LN, None, ALU.add))
                nc.vector.tensor_copy(newton[:], var_eps[:]).then_inc(var_ready, 1)
                dve.wait_ge(std_ready, n + 1)
                step(nc.vector.reciprocal(rstd[:], rstd[:]))
                step(nc.vector.tensor_tensor(newton[:], rstd[:], rstd[:], ALU.mult))
                step(nc.vector.tensor_tensor(newton[:], newton[:], var_eps[:], ALU.mult))
                step(nc.vector.tensor_scalar(newton[:], newton[:], -0.5, 1.5, ALU.mult, ALU.add))
                step(nc.vector.tensor_tensor(rstd[:], rstd[:], newton[:], ALU.mult))
                for r in range(RT):
                    step(nc.vector.tensor_scalar(dst[:, r, :], src[:, r, :], moments[:, r, 0:1], rstd[:, r:r + 1],
                                                 ALU.subtract, ALU.mult))

            def copy_transposes(first):
                for r in range(RT):
                    dve.wait_ge(t_mm, first + r + 1)
                    nc.vector.tensor_copy(rowsT[:, :, P * r:P * (r + 1)],
                                          bank[:, (first + r) % 2, 0:H].rearrange("p (k n) -> p k n", k=HALVES)
                                          ).then_inc(t_out, 1)

            for n in range(NV):
                nc.vector.memset(v[n][:], 1.0).then_inc(v_ones, 1)
            dve.wait_ge(x_in, 16)
            layernorm(x_sb, normed, 0)
            flat = normed[:].rearrange("p r h -> p (r h)")
            clean(flat, RT * H)
            nc.vector.tensor_copy(flat, fix[:]).then_inc(rows_ready, RT)
            copy_transposes(0)
            dve.wait_ge(small_in, SMALL)
            step(nc.vector.tensor_copy(attend[0:TT], mask_i[0:TT]))
            step(nc.vector.tensor_scalar(attend[0:TT], attend[0:TT], 0.5, None, ALU.is_gt))
            step(nc.vector.tensor_scalar(rscale[:], gates[:, 2:3], 0.0, 0.3, ALU.max, ALU.min))
            dve.wait_ge(q_out, 4)
            q_flat = qT[:].rearrange("p m r -> p (m r)")
            clean(q_flat, HALVES * ROWS)
            step(nc.vector.tensor_copy(q_flat, fix[:, 0:HALVES * ROWS]))
            dve.wait_ge(consts, CONSTS)

            def mask_of(b):
                after(dve, exp_out, HALVES * NT * b)
                cols = attend[0:TT, bass.ds(b * NT, NT)]
                nc.vector.tensor_scalar(mask_scale[0:TT], cols, HD ** -0.5, None, ALU.mult)
                nc.vector.tensor_scalar(mask_bias[0:TT], cols, 1.0, CLIP, ALU.subtract,
                                        ALU.mult).then_inc(mask_ready, 1)

            def build_qbd(b):
                after(dve, s_mm, HALVES * NT * b)
                for m in range(HALVES):
                    q = qT[:, m, bass.ds(b * S, S)].unsqueeze(1).broadcast_to([P, HH, S])
                    mask = head_mask[:].unsqueeze(2).broadcast_to([P, HH, S])
                    mm = nc.vector.tensor_tensor(qbd[:, m], q, mask, ALU.mult)
                mm.then_inc(qbd_ready, 1)

            def v_copy(b, i):
                dve.wait_ge(v_mm, NT * b + i + 1)
                after(dve, pv_mm, NT * b + i - NV + 1)
                nc.vector.tensor_tensor(v[i % NV][:, :, 0:HD],
                                        bank[0:TT, V_BANK, 0:H].rearrange("t (h d) -> t h d", h=NH),
                                        bv[0:TT].rearrange("t (h d) -> t h d", h=NH), ALU.add).then_inc(v_out, 1)

            def p_clip(b, i):
                for m in range(HALVES):
                    dve.wait_ge(exp_out, HALVES * (NT * b + i) + m + 1)
                    half = p[i % NP_][:, HALF * m:HALF * (m + 1)]
                    nc.vector.tensor_scalar(half, half, E_HI, E_LO, ALU.min, ALU.max).then_inc(p_out, 1)

            def acc_copy(b):
                dve.wait_ge(pv_mm, NT * (b + 1))
                after(dve, epi, 3 * b)
                nc.vector.tensor_copy(acc_sb[:], acc).then_inc(acc_out, 1)

            def den_copy(b):
                dve.wait_ge(den_mm, b + 1)
                nc.vector.tensor_copy(den_sb[:], den).then_inc(den_out, 1)

            def normalise(b):
                dve.wait_ge(den_out, b + 1)
                nc.vector.scalar_tensor_tensor(inv_den[:], den_sb[:], 1e-8, den_sb[:], ALU.mult,
                                               ALU.add).then_inc(epi, 1)
                dve.wait_ge(epi, 3 * b + 1)
                nc.vector.reciprocal(inv_den[:], inv_den[:]).then_inc(epi, 1)
                dve.wait_ge(epi, 3 * b + 2)
                nc.vector.tensor_tensor(ctxn[:, :, bass.ds(b * S, S)],
                                        acc_sb[:].rearrange("p (r s) -> p r s", r=SLOTS),
                                        inv_den[:].rearrange("p (r s) -> p r s", r=SLOTS),
                                        ALU.mult).then_inc(epi, 1)

            def batch(b, first, last):
                if not first:
                    acc_copy(b - 1)
                for i in range(NT):
                    v_copy(b, i)
                    if i == 0 and not first:
                        den_copy(b - 1)
                    p_clip(b, i)
                    if i == 1 and not first:
                        normalise(b - 1)
                if not last:
                    build_qbd(b + 1)
                    mask_of(b + 1)

            build_qbd(0)
            mask_of(0)
            dve.wait_ge(v_in, 32)
            batch(0, True, False)
            with dve.Fori(1, B - 1) as b:
                batch(b, False, False)
            batch(B - 1, False, True)
            acc_copy(B - 1)
            den_copy(B - 1)
            normalise(B - 1)

            dve.wait_ge(late_in, LATE)
            for r in range(RT):
                dve.wait_ge(o_mm, r + 1)
                nc.vector.tensor_tensor(normed[:, r, :], bank[:, r % 2, 0:H], bo[:], ALU.add).then_inc(o_out, 1)
            dve.wait_ge(o_out, RT)
            clean(flat, RT * H)
            step(nc.vector.tensor_scalar(flat, fix[:], rscale[:], None, ALU.mult))
            layernorm(normed, normed, 1)
            over_rows = [P, RT, H]
            step(nc.vector.tensor_tensor(normed[:], normed[:], gamma[:].unsqueeze(1).broadcast_to(over_rows), ALU.mult))
            step(nc.vector.tensor_tensor(normed[:], normed[:], beta[:].unsqueeze(1).broadcast_to(over_rows), ALU.add))
            dve.wait_ge(tanh_ready, 1)
            x_flat = x_sb[:].rearrange("p r h -> p (r h)")
            step(nc.vector.scalar_tensor_tensor(x_flat, flat, tanhs[:, 0:1], x_flat, ALU.mult, ALU.add))
            layernorm(x_sb, normed, 2)
            nc.vector.memset(y[:], 0.0).then_inc(rows_ready, RT)
            copy_transposes(RT)
            dve.wait_ge(r_mm, 1)
            by_row = [P, RT, NE]
            step(nc.vector.tensor_copy(logits[:], bank[:, 2, 0:RT * NE].rearrange("p (r e) -> p r e", r=RT)))
            step(nc.vector.tensor_reduce(row_max[:], logits[:], AX_X, ALU.max))
            nc.vector.tensor_tensor(logits[:], logits[:], row_max[:].unsqueeze(2).broadcast_to(by_row),
                                    ALU.subtract).then_inc(shifted, 1)
            dve.wait_ge(e_out, 1)
            step(nc.vector.tensor_reduce(row_sum[:], probs[:], AX_X, ALU.add))
            step(nc.vector.reciprocal(row_inv[:], row_sum[:]))
            step(nc.vector.tensor_tensor(probs[:], probs[:], row_inv[:].unsqueeze(2).broadcast_to(by_row), ALU.mult))
            pairs = [P, NE, NE]
            for r in range(RT):
                mine = probs[:, r, :].unsqueeze(2).broadcast_to(pairs)
                other = probs[:, r, :].unsqueeze(1).broadcast_to(pairs)
                step(nc.vector.tensor_tensor(above[:, r], other, mine, ALU.is_gt))
                step(nc.vector.tensor_tensor(ties[:, r], other, mine, ALU.is_equal))
                step(nc.vector.tensor_tensor(ties[:, r], ties[:, r], later_expert[:], ALU.mult))
            step(nc.vector.tensor_tensor(above[:], above[:], ties[:], ALU.add))
            step(nc.vector.tensor_reduce(weight[:], above[:], AX_X, ALU.add))
            step(nc.vector.tensor_scalar(weight[:], weight[:], 1.5, None, ALU.is_lt))
            step(nc.vector.tensor_tensor(weight[:], weight[:], probs[:], ALU.mult))
            step(nc.vector.tensor_reduce(row_sum[:], weight[:], AX_X, ALU.add))
            step(nc.vector.reciprocal(row_inv[:], row_sum[:]))
            step(nc.vector.tensor_tensor(weight[:], weight[:], row_inv[:].unsqueeze(2).broadcast_to(by_row), ALU.mult))

            def gate(e):
                for n in range(2):
                    s = 2 * e + n
                    dve.wait_ge(silu_out, s + 1)
                    if e >= 2:
                        dve.wait_ge(d_mm, RT * (e - 1))
                    nc.vector.tensor_tensor(act[:, e % 2, HALF * n:HALF * (n + 1)], silu[:, n, :],
                                            bank[:, 5 + 2 * n, 0:HALF], ALU.mult).then_inc(act_out, 1)

            gate(0)
            for e in range(NE):
                if e + 1 < NE:
                    gate(e + 1)
                for r in range(RT):
                    s = RT * e + r
                    dve.wait_ge(d_mm, s + 1)
                    after(dve, d_out, s - RT + 1)
                    nc.vector.scalar_tensor_tensor(y[:, r, :], bank[:, s % 2, 0:H], weight[:, r, e:e + 1], y[:, r, :],
                                                   ALU.mult, ALU.add).then_inc(d_out, 1)
            dve.wait_ge(d_out, NE * RT)
            nc.vector.scalar_tensor_tensor(flat, y[:].rearrange("p r h -> p (r h)"), tanhs[:, 1:2], x_flat,
                                           ALU.mult, ALU.add).then_inc(y_done, 1)


def kernel(x, ctx_2048, mask_BxS2_ik0, g_xattn, g_ffn, L0_xattn_Wq, L0_xattn_bq, L0_xattn_Wk, L0_xattn_bk,
           L0_xattn_Wv, L0_xattn_bv, L0_xattn_Wo, L0_xattn_bo, L0_xattn_ln_gamma, L0_xattn_ln_beta,
           L0_xattn_residual_scale, L0_ffn_router_gate, L0_ffn_expert_gate_up, L0_ffn_expert_down):
    import concourse.bacc as bacc
    from concourse.bass_utils import run_bass_kernel_spmd

    def rows_by_block(w):
        return np.asarray(w).T.reshape(HALVES, P, -1).transpose(1, 0, 2)

    ctx_l = np.asarray(ctx_2048).reshape(B, CHUNKS, CT, HALVES, P).transpose(0, 1, 4, 3, 2)
    mask_l = np.asarray(mask_BxS2_ik0).reshape(B * NT, TT).T
    wo_l = np.asarray(L0_xattn_Wo).T.reshape(SLOTS, GROUPS, HD, H).transpose(1, 2, 0, 3)
    gu_l = np.asarray(L0_ffn_expert_gate_up).reshape(NE, HALVES, P, FF, 2).transpose(2, 0, 1, 4, 3)
    arrays = {
        "x": np.asarray(x).reshape(ROWS, H), "ctx": ctx_l, "mask": mask_l,
        "gx": np.asarray(g_xattn), "gf": np.asarray(g_ffn),
        "wq": rows_by_block(L0_xattn_Wq), "bq": np.asarray(L0_xattn_bq).reshape(HALVES, P).T,
        "wk": rows_by_block(L0_xattn_Wk), "bk": np.asarray(L0_xattn_bk).reshape(HALVES, P).T,
        "wv": rows_by_block(L0_xattn_Wv), "bv": np.asarray(L0_xattn_bv),
        "wo": wo_l, "bo": np.asarray(L0_xattn_bo),
        "gamma": np.asarray(L0_xattn_ln_gamma), "beta": np.asarray(L0_xattn_ln_beta),
        "rs": np.asarray(L0_xattn_residual_scale).reshape(1),
        "router": rows_by_block(L0_ffn_router_gate), "gate_up": gu_l,
        "down": np.asarray(L0_ffn_expert_down).transpose(1, 0, 2),
    }
    arrays = {f"{k}_dram": np.ascontiguousarray(a) for k, a in arrays.items()}
    nc = bacc.Bacc("TRN2", target_bir_lowering=False, num_devices=1)
    args = [nc.dram_tensor(k, a.shape, mybir.dt.from_np(a.dtype), kind="ExternalInput").ap() for k, a in arrays.items()]
    args.append(nc.dram_tensor("out_dram", (ROWS, H), F32, kind="ExternalOutput").ap())
    flamingo(nc, *args)
    result = run_bass_kernel_spmd(nc, [arrays], core_ids=[0])
    return result.results[0]["out_dram"].reshape(B, S, H)
```

```python
from contextlib import ExitStack

import numpy as np

import concourse.bass as bass
from concourse import mybir

F32 = mybir.dt.float32
F32R = mybir.dt.float32r
U8 = mybir.dt.uint8
I32 = mybir.dt.int32
ALU = mybir.AluOpType
ACT = mybir.ActivationFunctionType
AX_X = mybir.AxisListType.X

P = 128
B, S, H = 16, 56, 256
T = 1500
NH, HD = 16, 16
HALVES = H // P
CHUNKS = 3
CT = T // CHUNKS
TT = 125
TPC = CT // TT
NT = T // TT
HH = NH // HALVES
HALF = HH * S
QG = 4
QH = NH // QG
QW = QH * S
ROWS = B * S
RT = ROWS // P
NV, NP_ = 4, 3
GROUPS = 4
SLOTS = NH // GROUPS
ACC = SLOTS * S
NE, FF = 8, 128
EPS_LN = 1e-5
CLIP = 50.0
E_HI, E_LO = float(np.exp(50.0)), float(np.exp(-50.0))
FMAX = float(np.finfo(np.float32).max)
LIM = 10000.0


def flamingo(nc, x_d, ctx_d, mask_d, gx_d, gf_d, wq_d, bq_d, wk_d, bk_d, wv_d, bv_d, wo_d, bo_d,
             gamma_d, beta_d, rs_d, router_d, gate_up_d, down_d, out_d):
    with ExitStack() as ctx:
        def sb(name, shape, dt=F32):
            return ctx.enter_context(nc.sbuf_tensor(name, shape, dt))

        def sem(name):
            return ctx.enter_context(nc.semaphore(name))

        def chunk_ahead(b, i, last, chunks):
            c = i // TPC + chunks
            if c < CHUNKS:
                return b, c
            return None if last else (b + 1, c - CHUNKS)

        def after(engine, semaphore, count):
            if isinstance(count, int) and count <= 0:
                return
            engine.wait_ge(semaphore, count)

        ident = sb("ident", [P, P])
        head_of, head_mask = sb("head_of", [P, HH]), sb("head_mask", [P, QH])
        den_select = sb("den_select", [P, P])
        later_expert = sb("later_expert", [P, NE, NE])
        wk_hi, wk_lo, wv_hi, wv_lo = (sb(n, [P, HALVES, H], F32R) for n in ("wk_hi", "wk_lo", "wv_hi", "wv_lo"))
        wo = sb("wo", [P, SLOTS, H])
        bq, bk = sb("bq", [P, HALVES]), sb("bk", [P // 2, QG])
        bv, bo, gamma, beta = (sb(n, [P, H]) for n in ("bv", "bo", "gamma", "beta"))
        router = sb("router", [P, HALVES, NE])
        q_or_ffn = sb("q_or_ffn", [P, 2 * QG * ROWS])
        q_rep = [q_or_ffn[:, QG * ROWS * n:QG * ROWS * (n + 1)].rearrange("p (g r) -> p g r", g=QG) for n in range(2)]
        gate_up = q_or_ffn[:, 0:NE * HALVES * 2 * FF].rearrange("p (e k g f) -> p e k g f", e=NE, k=HALVES, g=2)
        down = q_or_ffn[:, NE * HALVES * 2 * FF:NE * (HALVES * 2 * FF + H)].rearrange("p (e h) -> p e h", e=NE)
        gates = sb("gates", [P, 3])
        tanhs = sb("tanhs", [P, 2])
        rscale = sb("rscale", [P, 1])
        mask_i = sb("mask_i", [P, B * NT], I32)
        attend = sb("attend", [P, B * NT])
        mask_scale = sb("mask_scale", [P, 2, NT])
        mask_bias = sb("mask_bias", [P, 2, NT])
        x_sb = sb("x_sb", [P, RT, H])
        normed = sb("normed", [P, RT, H])
        fix = sb("fix", [P, RT * H])
        fix_neg = sb("fix_neg", [P, RT * H])
        finite = sb("finite", [P, RT * H], U8)
        stats = sb("stats", [P, RT, 6])
        moments = sb("moments", [P, RT, 2])
        var_eps, rstd, newton = sb("var_eps", [P, RT]), sb("rstd", [P, RT]), sb("newton", [P, RT])
        ctxn = sb("ctxn", [P, SLOTS, ROWS])
        rowsT, qT = ctxn[:, 0:HALVES, :], ctxn[:, HALVES:2 * HALVES, :]
        ctxT = [sb(f"ctxT{c}", [P, HALVES, CT]) for c in range(CHUNKS)]
        ctx_hi = [sb(f"ctx_hi{c}", [P, HALVES, CT], F32R) for c in range(CHUNKS)]
        ctx_lo = [sb(f"ctx_lo{c}", [P, HALVES, CT], F32R) for c in range(CHUNKS)]
        k_split = [sb(f"k_split{c}", [P, QG, CT], F32R) for c in range(CHUNKS)]
        qbd = [[sb(f"qbd{b}_{n}", [P, QG, QH, S], F32R) for n in ("hi", "lo")] for b in range(2)]
        v = [sb(f"v{n}", [TT, NH, HD + 1]) for n in range(NV)]
        p_or_other = [sb(f"p{n}", [P, NH * S]) for n in range(NP_)]
        p = [t[0:TT] for t in p_or_other]
        wq, wk, wv = (t[:, 0:HALVES * H].rearrange("p (k h) -> p k h", k=HALVES) for t in p_or_other)
        acc_sb, den_sb, inv_den = (sb(n, [P, ACC]) for n in ("acc_sb", "den_sb", "inv_den"))
        logits = sb("logits", [P, RT, NE])
        probs = sb("probs", [P, RT, NE])
        weight = sb("weight", [P, RT, NE])
        above, ties = (t[:, 0:RT * NE * NE].rearrange("p (r e f) -> p r e f", r=RT, e=NE) for t in p_or_other[0:2])
        row_max, row_sum, row_inv = sb("row_max", [P, RT]), sb("row_sum", [P, RT]), sb("row_inv", [P, RT])
        silu = sb("silu", [P, 2, HALF])
        act = fix_neg[:].rearrange("p (n r) -> p n r", n=2)
        y = fix[:].rearrange("p (r h) -> p r h", r=RT)

        bank = ctx.enter_context(nc.psum_tensor("bank", [P, 8, 512], F32))
        S_BANK = [0, 2]
        K_BANK = 4
        V_BANK = 6
        ACC_BANK = 7
        acc = bank[:, ACC_BANK, 0:ACC]
        den = bank[:, ACC_BANK, 256:256 + ACC]

        x_in, small_in, late_in = (sem(n) for n in ("x_in", "small_in", "late_in"))
        wq_in, wk_in, wv_in, bv_in = (sem(n) for n in ("wq_in", "wk_in", "wv_in", "bv_in"))
        ctx_in = [sem(f"ctx_in{c}") for c in range(CHUNKS)]
        consts = sem("consts")
        w_hi, w_lo = sem("w_hi"), sem("w_lo")
        hi_out, lo_out = sem("hi_out"), sem("lo_out")
        q_hi, q_lo, q_here = sem("q_hi"), sem("q_lo"), sem("q_here")
        acc_clear = sem("acc_clear")
        chain = sem("chain")
        var_ready, std_ready = sem("var_ready"), sem("std_ready")
        tanh_ready, wo_clear = sem("tanh_ready"), sem("wo_clear")
        rows_ready = sem("rows_ready")
        t_mm, t_out = sem("t_mm"), sem("t_out")
        q_mm, q_out, q_clean = sem("q_mm"), sem("q_out"), sem("q_clean")
        mask_ready, v_ones = sem("mask_ready"), sem("v_ones")
        qbd_clear, qbd_ready = sem("qbd_clear"), sem("qbd_ready")
        k_mm, k_hi, k_lo = sem("k_mm"), sem("k_hi"), sem("k_lo")
        v_mm, v_out = sem("v_mm"), sem("v_out")
        s_mm, exp_out, p_out = sem("s_mm"), sem("exp_out"), sem("p_out")
        pv_mm, acc_out, den_mm, den_out = sem("pv_mm"), sem("acc_out"), sem("den_mm"), sem("den_out")
        epi = sem("epi")
        o_mm, o_out = sem("o_mm"), sem("o_out")
        r_mm, r_out, e_out = sem("r_mm"), sem("r_out"), sem("e_out")
        shifted = sem("shifted")
        gu_mm, silu_out, act_out = sem("gu_mm"), sem("silu_out"), sem("act_out")
        d_mm, d_out = sem("d_mm"), sem("d_out")
        y_done, stored = sem("y_done"), sem("stored")

        block = ctx.enter_context(nc.Block())

        @block.sync
        def _(sp):
            sp.dma_start(x_sb[:], x_d.rearrange("(r p) h -> p r h", p=P)).then_inc(x_in, 16)
            sp.dma_start(wk, wk_d).then_inc(wk_in, 16)
            sp.dma_start(ctxT[0][:], ctx_d[0, 0]).then_inc(ctx_in[0], 16)
            sp.dma_start(wq, wq_d).then_inc(wq_in, 16)
            sp.dma_start(wv, wv_d).then_inc(wv_in, 16)
            sp.dma_start(bv[:], bv_d.partition_broadcast(P)).then_inc(bv_in, 16)
            for c in range(1, CHUNKS):
                sp.dma_start(ctxT[c][:], ctx_d[0, c]).then_inc(ctx_in[c], 16)
            for n, (ready, source) in enumerate(((q_hi, qT), (q_lo, fix_neg[:].rearrange("p (m r) -> p m r", m=HALVES)))):
                sp.wait_ge(ready, 1)
                for half in range(2):
                    for copy in range(2):
                        sp.dma_start(q_rep[n][64 * copy:64 * (copy + 1)].rearrange("p (m a) r -> p m a r", a=2)[:, :, half],
                                     source[64 * half:64 * (half + 1)]).then_inc(q_here, 16)
            sp.wait_ge(wo_clear, 1)
            for j in range(GROUPS):
                sp.dma_start(wo[2 * HD * j:2 * HD * j + HD], wo_d[j]).then_inc(late_in, 16)
            for tile, source in ((bo, bo_d), (gamma, gamma_d), (beta, beta_d)):
                sp.dma_start(tile[:], source.partition_broadcast(P)).then_inc(late_in, 16)
            sp.dma_start(router[:], router_d).then_inc(late_in, 16)

            with sp.Fori(1, B) as b:
                for c in range(CHUNKS):
                    sp.wait_ge(lo_out, (b - 1) * CHUNKS + c + 1)
                    sp.dma_start(ctxT[c][:], ctx_d[b, c]).then_inc(ctx_in[c], 16)
            sp.wait_ge(qbd_ready, 2 * B)
            sp.dma_start(gate_up, gate_up_d).then_inc(late_in, 16)
            sp.dma_start(down, down_d).then_inc(late_in, 16)
            sp.wait_ge(y_done, 1)
            sp.dma_start(out_d.rearrange("(r p) h -> p r h", p=P), normed[:]).then_inc(stored, 16)
            sp.wait_ge(stored, 16)
        LATE = 16 * (GROUPS + 6)

        @block.gpsimd
        def _(pool):
            for tile, source in ((bq, bq_d), (bk, bk_d)):
                pool.dma_start(tile[:], source).then_inc(small_in, 16)
            pool.dma_start(mask_i[0:TT], mask_d).then_inc(small_in, 16)
            for n, source in enumerate((gx_d, gf_d, rs_d)):
                pool.dma_start(gates[:, n:n + 1], source.partition_broadcast(P)).then_inc(small_in, 16)
            nc.gpsimd.memset(ident[:], 0.0).then_inc(consts, 1)
            nc.gpsimd.memset(head_of[:], 1.0).then_inc(consts, 1)
            nc.gpsimd.memset(den_select[:], 0.0).then_inc(consts, 1)
            nc.gpsimd.memset(later_expert[:], 1.0).then_inc(consts, 1)
            nc.gpsimd.memset(wo[:], 0.0).then_inc(wo_clear, 1)
            pool.wait_ge(consts, 4)
            nc.gpsimd.affine_select(out=ident[:], in_=ident[:], compare_op=ALU.not_equal, fill=1.0, base=0,
                                    pattern=[[-1, P]], channel_multiplier=1).then_inc(consts, 1)
            nc.gpsimd.affine_select(out=head_of[:], in_=head_of[:], compare_op=ALU.is_ge, fill=0.0, base=0,
                                    pattern=[[-HD, HH]], channel_multiplier=1).then_inc(consts, 1)
            pool.wait_ge(consts, 6)
            nc.gpsimd.affine_select(out=head_of[:], in_=head_of[:], compare_op=ALU.is_ge, fill=0.0, base=HD - 1,
                                    pattern=[[HD, HH]], channel_multiplier=-1).then_inc(consts, 1)
            pool.wait_ge(consts, 7)
            nc.gpsimd.tensor_tensor(head_mask[:], head_of[:, 0:QH], head_of[:, QH:HH], ALU.add).then_inc(consts, 1)
            sel = den_select[:].rearrange("k (j m) -> k j m", j=GROUPS)
            nc.gpsimd.affine_select(out=sel, in_=sel, compare_op=ALU.not_equal, fill=1.0, base=-HD,
                                    pattern=[[-2 * HD, GROUPS], [0, 2 * HD]], channel_multiplier=1).then_inc(consts, 1)
            nc.gpsimd.affine_select(out=later_expert[:], in_=later_expert[:], compare_op=ALU.is_ge, fill=0.0,
                                    base=-1, pattern=[[1, NE], [-1, NE]], channel_multiplier=0).then_inc(consts, 1)
        CONSTS = 10
        SMALL = 16 * 6

        @block.tensor
        def _(pe):
            def transposes(first):
                for r in range(RT):
                    pe.wait_ge(rows_ready, first + r + 1)
                    if first + r >= 2:
                        pe.wait_ge(t_out, first + r - 1)
                    for k in range(HALVES):
                        mm = nc.tensor.transpose(bank[:, (first + r) % 2, P * k:P * (k + 1)],
                                                 normed[:, r, P * k:P * (k + 1)], ident[:])
                    mm.then_inc(t_mm, 1)

            def k_proj(b, c, m):
                if m == 0:
                    pe.wait_ge(hi_out, CHUNKS * b + c + 1)
                    pe.wait_ge(lo_out, CHUNKS * b + c + 1)
                after(pe, k_lo, QG * (CHUNKS * b + c - 1) + 2 * (m + 1))
                terms = [(w, t, k) for w, t in ((wk_lo, ctx_hi), (wk_hi, ctx_lo), (wk_hi, ctx_hi)) for k in range(HALVES)]
                for n, (w, t, k) in enumerate(terms):
                    mm = nc.tensor.matmul(bank[:, K_BANK + m, 0:CT], w[:, k, P * m:P * (m + 1)], t[c][:, k, :],
                                          start=(n == 0), stop=(n == len(terms) - 1))
                mm.then_inc(k_mm, 1)

            def v_proj(b, i):
                c, t0 = i // TPC, TT * (i % TPC)
                after(pe, v_out, NT * b + i)
                terms = [(t, w, k) for t, w in ((ctx_lo, wv_hi), (ctx_hi, wv_lo), (ctx_hi, wv_hi)) for k in range(HALVES)]
                for n, (t, w, k) in enumerate(terms):
                    mm = nc.tensor.matmul(bank[0:TT, V_BANK, 0:H], t[c][:, k, t0:t0 + TT], w[:, k, :],
                                          start=(n == 0), stop=(n == len(terms) - 1))
                mm.then_inc(v_mm, 1)

            def scores(b, parity, i):
                c, t0 = i // TPC, TT * (i % TPC)
                if i == 0:
                    pe.wait_ge(qbd_ready, 2 * (b + 1))
                if i % TPC == 0:
                    pe.wait_ge(k_lo, QG * (CHUNKS * b + c + 1))
                after(pe, exp_out, NT * b + i - 1)
                for g in range(QG):
                    col = QW * (g % 2)
                    for n in range(2):
                        mm = nc.tensor.matmul(bank[0:TT, S_BANK[i % 2] + g // 2, col:col + QW],
                                              k_split[c][:, g, t0:t0 + TT], qbd[parity][n][:, g],
                                              start=(n == 0), stop=(n == 1))
                mm.then_inc(s_mm, 1)

            def p_v(b, i):
                pe.wait_ge(v_out, NT * b + i + 1)
                if i == 0:
                    after(pe, den_out, b)
                for slot in range(SLOTS):
                    for j in range(GROUPS):
                        h = GROUPS * slot + j
                        if h == 0:
                            pe.wait_ge(p_out, NT * b + i + 1)
                        mm = nc.tensor.matmul(acc[2 * HD * j:2 * HD * j + HD + 1, S * slot:S * (slot + 1)],
                                              v[i % NV][:, h, 0:HD + 1], p[i % NP_][:, S * h:S * (h + 1)],
                                              start=(i == 0 and slot == 0), stop=(i == NT - 1),
                                              skip_group_check=True)
                mm.then_inc(pv_mm, 1)

            def denominators(b):
                pe.wait_ge(acc_out, b + 1)
                nc.tensor.matmul(den, den_select[:], acc_sb[:], start=True, stop=True,
                                 skip_group_check=True).then_inc(den_mm, 1)

            def batch(b, parity, first, last):
                for i in range(NT):
                    scores(b, parity, i)
                    if i == 1 and not first:
                        denominators(b - 1)
                    v_proj(b, i)
                    ahead = chunk_ahead(b, i, last, 1)
                    if i % TPC in (1, 2) and ahead:
                        k_proj(*ahead, i % TPC - 1)
                    if i > 0:
                        p_v(b, i - 1)
                    elif not first:
                        p_v(b - 1, NT - 1)

            pe.wait_ge(consts, CONSTS)
            pe.wait_ge(w_hi, 2)
            pe.wait_ge(w_lo, 2)
            k_proj(0, 0, 0)
            k_proj(0, 0, 1)
            transposes(0)
            pe.wait_ge(wq_in, 16)
            pe.wait_ge(t_out, RT)
            for n in range(2):
                for m in range(HALVES):
                    if n:
                        pe.wait_ge(q_out, m + 1)
                    for k in range(HALVES):
                        mm = nc.tensor.matmul(bank[:, 2 + m, 0:HALF], wq[:, k, P * m:P * (m + 1)],
                                              rowsT[:, k, HALF * n:HALF * (n + 1)],
                                              start=(k == 0), stop=(k == HALVES - 1))
                    mm.then_inc(q_mm, 1)
            pe.wait_ge(q_out, 4)
            pe.wait_ge(v_ones, NV)
            pe.wait_ge(acc_clear, 1)
            batch(0, 0, True, False)
            with pe.Fori(0, B // 2 - 1) as pair:
                batch(2 * pair + 1, 1, False, False)
                batch(2 * pair + 2, 0, False, False)
            batch(B - 1, 1, False, True)
            p_v(B - 1, NT - 1)
            denominators(B - 1)

            pe.wait_ge(late_in, LATE)
            pe.wait_ge(epi, 3 * B)
            for r in range(RT):
                if r >= 2:
                    pe.wait_ge(o_out, r - 1)
                for slot in range(SLOTS):
                    mm = nc.tensor.matmul(bank[:, r % 2, 0:H], ctxn[:, slot, P * r:P * (r + 1)], wo[:, slot, :],
                                          start=(slot == 0), stop=(slot == SLOTS - 1))
                mm.then_inc(o_mm, 1)
            transposes(RT)
            pe.wait_ge(t_out, 2 * RT)
            for r in range(RT):
                for k in range(HALVES):
                    mm = nc.tensor.matmul(bank[:, 2, NE * r:NE * (r + 1)], rowsT[:, k, P * r:P * (r + 1)],
                                          router[:, k, :], start=(k == 0), stop=(k == HALVES - 1))
            mm.then_inc(r_mm, 1)

            def expert_in(e):
                for n in range(2):
                    step = 2 * e + n
                    if step >= 2:
                        pe.wait_ge(act_out, step - 1)
                    for g in range(2):
                        for k in range(HALVES):
                            mm = nc.tensor.matmul(bank[:, 4 + 2 * n + g, 0:HALF], gate_up[:, e, k, g, :],
                                                  rowsT[:, k, HALF * n:HALF * (n + 1)],
                                                  start=(k == 0), stop=(k == HALVES - 1))
                    mm.then_inc(gu_mm, 1)

            def expert_out(e):
                for r in range(RT):
                    step = RT * e + r
                    if r == 0:
                        pe.wait_ge(act_out, 2 * e + 1)
                    if r == RT // 2:
                        pe.wait_ge(act_out, 2 * e + 2)
                    if step >= 2:
                        pe.wait_ge(d_out, step - 1)
                    nc.tensor.matmul(bank[:, step % 2, 0:H], act[:, e % 2, P * r:P * (r + 1)], down[:, e, :],
                                     start=True, stop=True).then_inc(d_mm, 1)

            expert_in(0)
            for e in range(NE):
                if e + 1 < NE:
                    expert_in(e + 1)
                expert_out(e)

        @block.scalar
        def _(act_e):
            def sqrt_var(n):
                act_e.wait_ge(var_ready, n + 1)
                nc.scalar.activation(rstd[:], var_eps[:], ACT.Sqrt).then_inc(std_ready, 1)

            def k_high(b, c, m):
                act_e.wait_ge(k_mm, HALVES * (CHUNKS * b + c) + m + 1)
                after(act_e, s_mm, NT * (b - 1) + TPC * (c + 1))
                for a in range(2):
                    g = 2 * m + a
                    nc.scalar.activation(k_split[c][0:64, g, :], bank[64 * a:64 * (a + 1), K_BANK + m, 0:CT],
                                         ACT.Identity, bias=bk[:, g:g + 1]).then_inc(k_hi, 1)

            def ctx_high(b, c):
                act_e.wait_ge(ctx_in[c], 16 * b + 16)
                after(act_e, v_mm, (b - 1) * NT + TPC * (c + 1))
                nc.scalar.copy(ctx_hi[c][:], ctxT[c][:]).then_inc(hi_out, 1)

            def exps(b, parity, i):
                after(act_e, pv_mm, NT * b + i - NP_ + 1)
                if i == 0:
                    act_e.wait_ge(mask_ready, b + 1)
                act_e.wait_ge(s_mm, NT * b + i + 1)
                banks = bank[0:TT, S_BANK[i % 2]:S_BANK[i % 2] + HALVES, 0:HALF]
                nc.scalar.activation(p[i % NP_].rearrange("t (m n) -> t m n", m=HALVES), banks, ACT.Exp,
                                     bias=mask_bias[0:TT, parity, i:i + 1],
                                     scale=mask_scale[0:TT, parity, i:i + 1]).then_inc(exp_out, 1)

            def batch(b, parity, last):
                for i in range(NT):
                    exps(b, parity, i)
                    ahead = chunk_ahead(b, i, last, 1)
                    if i % TPC in (1, 2) and ahead:
                        k_high(*ahead, i % TPC - 1)
                    ahead = chunk_ahead(b, i, last, 2)
                    if i % TPC == 3 and ahead:
                        ctx_high(*ahead)

            act_e.wait_ge(wk_in, 16)
            nc.scalar.copy(wk_hi[:], wk).then_inc(w_hi, 1)
            ctx_high(0, 0)
            ctx_high(0, 1)
            act_e.wait_ge(wv_in, 16)
            nc.scalar.copy(wv_hi[:], wv).then_inc(w_hi, 1)
            act_e.wait_ge(small_in, SMALL)
            sqrt_var(0)
            k_high(0, 0, 0)
            k_high(0, 0, 1)
            nc.scalar.activation(tanhs[:], gates[:, 0:2], ACT.Tanh).then_inc(tanh_ready, 1)
            for n in range(2):
                for m in range(HALVES):
                    act_e.wait_ge(q_mm, 2 * n + m + 1)
                    nc.scalar.activation(qT[:, m, HALF * n:HALF * (n + 1)], bank[:, 2 + m, 0:HALF], ACT.Identity,
                                         bias=bq[:, m:m + 1]).then_inc(q_out, 1)
            batch(0, 0, False)
            with act_e.Fori(0, B // 2 - 1) as pair:
                batch(2 * pair + 1, 1, False)
                batch(2 * pair + 2, 0, False)
            batch(B - 1, 1, True)

            sqrt_var(1)
            sqrt_var(2)
            act_e.wait_ge(shifted, 1)
            nc.scalar.activation(probs[:], logits[:], ACT.Exp).then_inc(e_out, 1)
            for step in range(2 * NE):
                act_e.wait_ge(gu_mm, step + 1)
                if step >= 2:
                    act_e.wait_ge(act_out, step - 1)
                nc.scalar.activation(silu[:, step % 2, :], bank[:, 4 + 2 * (step % 2), 0:HALF],
                                     ACT.Silu).then_inc(silu_out, 1)

        @block.vector
        def _(dve):
            count = [0]

            def step(ins):
                count[0] += 1
                ins.then_inc(chain, 1)
                dve.wait_ge(chain, count[0])

            def clean(t, n):
                f, g, m = fix[:, 0:n], fix_neg[:, 0:n], finite[:, 0:n]
                step(nc.vector.tensor_scalar(f, t, 0.0, LIM, ALU.max, ALU.min))
                step(nc.vector.tensor_scalar(g, t, 0.0, -LIM, ALU.min, ALU.max))
                step(nc.vector.tensor_scalar(m, t, 0.0, 0.0, ALU.mult, ALU.is_equal))
                step(nc.vector.tensor_tensor(f, f, g, ALU.add))
                step(nc.vector.copy_predicated(f, m, t))

            def layernorm(src, dst, n):
                for r in range(RT):
                    step(nc.vector.bn_stats(stats[:, r, :], src[:, r, :]))
                for r in range(RT):
                    step(nc.vector.bn_aggr(moments[:, r, :], stats[:, r, :]))
                step(nc.vector.tensor_scalar(var_eps[:], moments[:, :, 1], EPS_LN, None, ALU.add))
                nc.vector.tensor_copy(newton[:], var_eps[:]).then_inc(var_ready, 1)
                dve.wait_ge(std_ready, n + 1)
                step(nc.vector.reciprocal(rstd[:], rstd[:]))
                step(nc.vector.tensor_tensor(newton[:], rstd[:], rstd[:], ALU.mult))
                step(nc.vector.tensor_tensor(newton[:], newton[:], var_eps[:], ALU.mult))
                step(nc.vector.tensor_scalar(newton[:], newton[:], -0.5, 1.5, ALU.mult, ALU.add))
                step(nc.vector.tensor_tensor(rstd[:], rstd[:], newton[:], ALU.mult))
                for r in range(RT):
                    step(nc.vector.tensor_scalar(dst[:, r, :], src[:, r, :], moments[:, r, 0:1], rstd[:, r:r + 1],
                                                 ALU.subtract, ALU.mult))

            def ctx_low(b, c):
                dve.wait_ge(hi_out, CHUNKS * b + c + 1)
                after(dve, v_mm, (b - 1) * NT + TPC * (c + 1))
                nc.vector.tensor_tensor(ctx_lo[c][:], ctxT[c][:], ctx_hi[c][:].bitcast(F32),
                                        ALU.subtract).then_inc(lo_out, 1)

            def k_low(b, c, m):
                after(dve, s_mm, NT * (b - 1) + TPC * (c + 1))
                for a in range(2):
                    g = 2 * m + a
                    dve.wait_ge(k_hi, QG * (CHUNKS * b + c) + g + 1)
                    nc.vector.scalar_tensor_tensor(k_split[c][64:128, g, :], bank[64 * a:64 * (a + 1), K_BANK + m, 0:CT],
                                                   bk[:, g:g + 1], k_split[c][0:64, g, :].bitcast(F32),
                                                   ALU.add, ALU.subtract).then_inc(k_lo, 1)

            def copy_transposes(first):
                for r in range(RT):
                    dve.wait_ge(t_mm, first + r + 1)
                    nc.vector.tensor_copy(rowsT[:, :, P * r:P * (r + 1)],
                                          bank[:, (first + r) % 2, 0:H].rearrange("p (k n) -> p k n", k=HALVES)
                                          ).then_inc(t_out, 1)

            nc.vector.memset(acc, 0.0).then_inc(acc_clear, 1)
            for n in range(NV):
                nc.vector.memset(v[n][:], 1.0).then_inc(v_ones, 1)
            dve.wait_ge(x_in, 16)
            for n, (low, raw, high) in enumerate(((wk_lo, wk, wk_hi), (wv_lo, wv, wv_hi))):
                dve.wait_ge(w_hi, n + 1)
                nc.vector.tensor_tensor(low[:], raw, high[:].bitcast(F32), ALU.subtract).then_inc(w_lo, 1)
                if n == 0:
                    ctx_low(0, 0)
                    ctx_low(0, 1)
            layernorm(x_sb, normed, 0)
            flat = normed[:].rearrange("p r h -> p (r h)")
            clean(flat, RT * H)
            nc.vector.tensor_copy(flat, fix[:]).then_inc(rows_ready, RT)
            copy_transposes(0)
            dve.wait_ge(small_in, SMALL)
            step(nc.vector.tensor_copy(attend[0:TT], mask_i[0:TT]))
            step(nc.vector.tensor_scalar(attend[0:TT], attend[0:TT], 0.5, None, ALU.is_gt))
            step(nc.vector.tensor_scalar(rscale[:], gates[:, 2:3], 0.0, 0.3, ALU.max, ALU.min))
            k_low(0, 0, 0)
            k_low(0, 0, 1)
            dve.wait_ge(q_out, 4)
            q_flat = qT.rearrange("p m r -> p (m r)")
            clean(q_flat, HALVES * ROWS)
            nc.vector.tensor_copy(q_flat.bitcast(F32R), fix[:]).then_inc(q_hi, 1)
            dve.wait_ge(q_hi, 1)
            nc.vector.tensor_tensor(fix_neg[:], fix[:], q_flat, ALU.subtract).then_inc(q_lo, 1)
            dve.wait_ge(q_here, 16 * 8)
            dve.wait_ge(consts, CONSTS)

            def mask_of(b, parity):
                after(dve, exp_out, NT * (b - 1))
                cols = attend[0:TT, bass.ds(b * NT, NT)]
                nc.vector.tensor_scalar(mask_scale[0:TT, parity], cols, HD ** -0.5, None, ALU.mult)
                nc.vector.tensor_scalar(mask_bias[0:TT, parity], cols, 1.0, CLIP, ALU.subtract,
                                        ALU.mult).then_inc(mask_ready, 1)

            def build_qbd(b, parity, n):
                after(dve, s_mm, NT * (b - 1))
                q = q_rep[n][:, :, bass.ds(b * S, S)].unsqueeze(2).broadcast_to([P, QG, QH, S])
                mask = head_mask[:].unsqueeze(1).unsqueeze(3).broadcast_to([P, QG, QH, S])
                nc.vector.tensor_tensor(qbd[parity][n][:], q, mask, ALU.mult).then_inc(qbd_ready, 1)

            def v_copy(b, i):
                dve.wait_ge(v_mm, NT * b + i + 1)
                after(dve, pv_mm, NT * b + i - NV + 1)
                nc.vector.tensor_tensor(v[i % NV][:, :, 0:HD],
                                        bank[0:TT, V_BANK, 0:H].rearrange("t (h d) -> t h d", h=NH),
                                        bv[0:TT].rearrange("t (h d) -> t h d", h=NH), ALU.add).then_inc(v_out, 1)

            def p_clip(b, i):
                dve.wait_ge(exp_out, NT * b + i + 1)
                tile = p[i % NP_]
                nc.vector.tensor_scalar(tile, tile, E_HI, E_LO, ALU.min, ALU.max).then_inc(p_out, 1)

            def acc_copy(b):
                dve.wait_ge(pv_mm, NT * (b + 1))
                nc.vector.tensor_copy(acc_sb[:], acc).then_inc(acc_out, 1)

            def den_copy(b):
                dve.wait_ge(den_mm, b + 1)
                nc.vector.tensor_copy(den_sb[:], den).then_inc(den_out, 1)

            def normalise(b):
                dve.wait_ge(den_out, b + 1)
                nc.vector.scalar_tensor_tensor(inv_den[:], den_sb[:], 1e-8, den_sb[:], ALU.mult,
                                               ALU.add).then_inc(epi, 1)
                dve.wait_ge(epi, 3 * b + 1)
                nc.vector.reciprocal(inv_den[:], inv_den[:]).then_inc(epi, 1)
                dve.wait_ge(epi, 3 * b + 2)
                nc.vector.tensor_tensor(ctxn[:, :, bass.ds(b * S, S)],
                                        acc_sb[:].rearrange("p (r s) -> p r s", r=SLOTS),
                                        inv_den[:].rearrange("p (r s) -> p r s", r=SLOTS),
                                        ALU.mult).then_inc(epi, 1)

            def batch(b, parity, first, last):
                for i in range(NT):
                    v_copy(b, i)
                    if not first:
                        if i == 0:
                            acc_copy(b - 1)
                        if i == 1:
                            den_copy(b - 1)
                    p_clip(b, i)
                    if i == TPC and not first:
                        normalise(b - 1)
                    ahead = chunk_ahead(b, i, last, 1)
                    if i % TPC in (1, 2) and ahead:
                        k_low(*ahead, i % TPC - 1)
                    ahead = chunk_ahead(b, i, last, 2)
                    if i % TPC == 3 and ahead:
                        ctx_low(*ahead)
                    if i == 0 and not last:
                        mask_of(b + 1, 1 - parity)
                        build_qbd(b + 1, 1 - parity, 0)
                    if i == 2 * TPC and not last:
                        build_qbd(b + 1, 1 - parity, 1)

            build_qbd(0, 0, 0)
            build_qbd(0, 0, 1)
            mask_of(0, 0)
            dve.wait_ge(bv_in, 16)
            batch(0, 0, True, False)
            with dve.Fori(0, B // 2 - 1) as pair:
                batch(2 * pair + 1, 1, False, False)
                batch(2 * pair + 2, 0, False, False)
            batch(B - 1, 1, False, True)
            acc_copy(B - 1)
            den_copy(B - 1)
            normalise(B - 1)

            dve.wait_ge(late_in, LATE)
            for r in range(RT):
                dve.wait_ge(o_mm, r + 1)
                nc.vector.tensor_tensor(normed[:, r, :], bank[:, r % 2, 0:H], bo[:], ALU.add).then_inc(o_out, 1)
            dve.wait_ge(o_out, RT)
            clean(flat, RT * H)
            step(nc.vector.tensor_scalar(flat, fix[:], rscale[:], None, ALU.mult))
            layernorm(normed, normed, 1)
            over_rows = [P, RT, H]
            step(nc.vector.tensor_tensor(normed[:], normed[:], gamma[:].unsqueeze(1).broadcast_to(over_rows), ALU.mult))
            step(nc.vector.tensor_tensor(normed[:], normed[:], beta[:].unsqueeze(1).broadcast_to(over_rows), ALU.add))
            dve.wait_ge(tanh_ready, 1)
            x_flat = x_sb[:].rearrange("p r h -> p (r h)")
            step(nc.vector.scalar_tensor_tensor(x_flat, flat, tanhs[:, 0:1], x_flat, ALU.mult, ALU.add))
            layernorm(x_sb, normed, 2)
            nc.vector.memset(y[:], 0.0).then_inc(rows_ready, RT)
            copy_transposes(RT)
            dve.wait_ge(r_mm, 1)
            by_row = [P, RT, NE]
            step(nc.vector.tensor_copy(logits[:], bank[:, 2, 0:RT * NE].rearrange("p (r e) -> p r e", r=RT)))
            step(nc.vector.tensor_reduce(row_max[:], logits[:], AX_X, ALU.max))
            nc.vector.tensor_tensor(logits[:], logits[:], row_max[:].unsqueeze(2).broadcast_to(by_row),
                                    ALU.subtract).then_inc(shifted, 1)
            dve.wait_ge(e_out, 1)
            step(nc.vector.tensor_reduce(row_sum[:], probs[:], AX_X, ALU.add))
            step(nc.vector.reciprocal(row_inv[:], row_sum[:]))
            step(nc.vector.tensor_tensor(probs[:], probs[:], row_inv[:].unsqueeze(2).broadcast_to(by_row), ALU.mult))
            pairs = [P, NE, NE]
            for r in range(RT):
                mine = probs[:, r, :].unsqueeze(2).broadcast_to(pairs)
                other = probs[:, r, :].unsqueeze(1).broadcast_to(pairs)
                step(nc.vector.tensor_tensor(above[:, r], other, mine, ALU.is_gt))
                step(nc.vector.tensor_tensor(ties[:, r], other, mine, ALU.is_equal))
                step(nc.vector.tensor_tensor(ties[:, r], ties[:, r], later_expert[:], ALU.mult))
            step(nc.vector.tensor_tensor(above, above, ties, ALU.add))
            step(nc.vector.tensor_reduce(weight[:], above, AX_X, ALU.add))
            step(nc.vector.tensor_scalar(weight[:], weight[:], 1.5, None, ALU.is_lt))
            step(nc.vector.tensor_tensor(weight[:], weight[:], probs[:], ALU.mult))
            step(nc.vector.tensor_reduce(row_sum[:], weight[:], AX_X, ALU.add))
            step(nc.vector.reciprocal(row_inv[:], row_sum[:]))
            step(nc.vector.tensor_tensor(weight[:], weight[:], row_inv[:].unsqueeze(2).broadcast_to(by_row), ALU.mult))

            def gate(e):
                for n in range(2):
                    s = 2 * e + n
                    dve.wait_ge(silu_out, s + 1)
                    if e >= 2:
                        dve.wait_ge(d_mm, RT * (e - 1))
                    nc.vector.tensor_tensor(act[:, e % 2, HALF * n:HALF * (n + 1)], silu[:, n, :],
                                            bank[:, 5 + 2 * n, 0:HALF], ALU.mult).then_inc(act_out, 1)

            gate(0)
            for e in range(NE):
                if e + 1 < NE:
                    gate(e + 1)
                for r in range(RT):
                    s = RT * e + r
                    dve.wait_ge(d_mm, s + 1)
                    after(dve, d_out, s - RT + 1)
                    nc.vector.scalar_tensor_tensor(y[:, r, :], bank[:, s % 2, 0:H], weight[:, r, e:e + 1], y[:, r, :],
                                                   ALU.mult, ALU.add).then_inc(d_out, 1)
            dve.wait_ge(d_out, NE * RT)
            nc.vector.scalar_tensor_tensor(flat, y[:].rearrange("p r h -> p (r h)"), tanhs[:, 1:2], x_flat,
                                           ALU.mult, ALU.add).then_inc(y_done, 1)


def kernel(x, ctx_2048, mask_BxS2_ik0, g_xattn, g_ffn, L0_xattn_Wq, L0_xattn_bq, L0_xattn_Wk, L0_xattn_bk,
           L0_xattn_Wv, L0_xattn_bv, L0_xattn_Wo, L0_xattn_bo, L0_xattn_ln_gamma, L0_xattn_ln_beta,
           L0_xattn_residual_scale, L0_ffn_router_gate, L0_ffn_expert_gate_up, L0_ffn_expert_down):
    import concourse.bacc as bacc
    from concourse.bass_utils import run_bass_kernel_spmd

    def rows_by_block(w):
        return np.asarray(w).T.reshape(HALVES, P, -1).transpose(1, 0, 2)

    ctx_l = np.asarray(ctx_2048).reshape(B, CHUNKS, CT, HALVES, P).transpose(0, 1, 4, 3, 2)
    mask_l = np.asarray(mask_BxS2_ik0).reshape(B * NT, TT).T
    wo_l = np.asarray(L0_xattn_Wo).T.reshape(SLOTS, GROUPS, HD, H).transpose(1, 2, 0, 3)
    gu_l = np.asarray(L0_ffn_expert_gate_up).reshape(NE, HALVES, P, FF, 2).transpose(2, 0, 1, 4, 3)
    arrays = {
        "x": np.asarray(x).reshape(ROWS, H), "ctx": ctx_l, "mask": mask_l,
        "gx": np.asarray(g_xattn), "gf": np.asarray(g_ffn),
        "wq": rows_by_block(L0_xattn_Wq), "bq": np.asarray(L0_xattn_bq).reshape(HALVES, P).T,
        "wk": rows_by_block(L0_xattn_Wk), "bk": np.asarray(L0_xattn_bk).reshape(QG, P // 2).T,
        "wv": rows_by_block(L0_xattn_Wv), "bv": np.asarray(L0_xattn_bv),
        "wo": wo_l, "bo": np.asarray(L0_xattn_bo),
        "gamma": np.asarray(L0_xattn_ln_gamma), "beta": np.asarray(L0_xattn_ln_beta),
        "rs": np.asarray(L0_xattn_residual_scale).reshape(1),
        "router": rows_by_block(L0_ffn_router_gate), "gate_up": gu_l,
        "down": np.asarray(L0_ffn_expert_down).transpose(1, 0, 2),
    }
    arrays = {f"{k}_dram": np.ascontiguousarray(a) for k, a in arrays.items()}
    nc = bacc.Bacc("TRN2", target_bir_lowering=False, num_devices=1)
    args = [nc.dram_tensor(k, a.shape, mybir.dt.from_np(a.dtype), kind="ExternalInput").ap() for k, a in arrays.items()]
    args.append(nc.dram_tensor("out_dram", (ROWS, H), F32, kind="ExternalOutput").ap())
    flamingo(nc, *args)
    result = run_bass_kernel_spmd(nc, [arrays], core_ids=[0])
    return result.results[0]["out_dram"].reshape(B, S, H)
```

```python
from contextlib import ExitStack

import numpy as np

import concourse.bass as bass
from concourse import mybir

F32 = mybir.dt.float32
F32R = mybir.dt.float32r
U8 = mybir.dt.uint8
I32 = mybir.dt.int32
ALU = mybir.AluOpType
ACT = mybir.ActivationFunctionType
AX_X = mybir.AxisListType.X

P = 128
B, S, H = 16, 56, 256
T = 1500
NH, HD = 16, 16
HALVES = H // P
CHUNKS = 6
CT = T // CHUNKS
TT = 125
TPC = CT // TT
NT = T // TT
HH = NH // HALVES
HALF = HH * S
QG = 4
QH = NH // QG
QW = QH * S
ROWS = B * S
PAIRS = B // 2
R2 = 2 * S
RPH = PAIRS // 2
HR = ROWS // 2
GROUPS = 4
SLOTS = NH // GROUPS
ACC = SLOTS * S
NE, FF = 8, 128
EPS_LN = 1e-5
CLIP = 50.0
E_HI, E_LO = float(np.exp(50.0)), float(np.exp(-50.0))
LIM = 10000.0


def flamingo(nc, x_d, ctx_d, mask_d, gx_d, gf_d, wq_d, bq_d, wk_d, bk_d, wv_d, bv_d, wo_d, bo_d,
             gamma_d, beta_d, rs_d, router_d, gate_up_d, down_d, out_d):
    with ExitStack() as ctx:
        def sb(name, shape, dt=F32):
            return ctx.enter_context(nc.sbuf_tensor(name, shape, dt))

        def sem(name):
            return ctx.enter_context(nc.semaphore(name))

        def after(engine, semaphore, count):
            if isinstance(count, int) and count <= 0:
                return
            engine.wait_ge(semaphore, count)

        ident = sb("ident", [P, P])
        code_weights = sb("code_weights", [B * CHUNKS, 2 * B])
        ones = sb("ones", [P, 1])
        head_of, head_mask = sb("head_of", [P, HH]), sb("head_mask", [P, QH])
        den_select = sb("den_select", [P, P])
        later_expert = sb("later_expert", [P, NE, NE])
        eps, minus_half, three_halves = (sb(n, [R2, PAIRS]) for n in ("eps", "minus_half", "three_halves"))
        spare, passed = sb("spare", [P, 2]), sb("passed", [P, CHUNKS])
        wk_hi, wk_lo, wv_hi, wv_lo = (sb(n, [P, HALVES, H], F32R) for n in ("wk_hi", "wk_lo", "wv_hi", "wv_lo"))
        wq, wk, wv = (sb(n, [P, HALVES, H]) for n in ("wq", "wk", "wv"))
        wo = sb("wo", [P, SLOTS, H])
        bq, bk = sb("bq", [P, HALVES]), sb("bk", [P // 2, QG])
        bv, bo, gamma, beta = (sb(n, [P, H]) for n in ("bv", "bo", "gamma", "beta"))
        router = sb("router", [P, HALVES, NE])
        gate_up, down = sb("gate_up", [P, NE, HALVES, 2, FF]), sb("down", [P, NE, H])
        gates = sb("gates", [P, 3])
        tanhs = sb("tanhs", [P, 2])
        rscale = sb("rscale", [P, 1])
        mask_i = sb("mask_i", [P, B * NT], I32)
        attend = sb("attend", [P, B * NT])
        chunk_any = sb("chunk_any", [P, B * CHUNKS])
        general = sb("general", [B * CHUNKS, 1])
        code_f, code = sb("code_f", [1, 2 * B]), sb("code", [1, B], I32)
        masked_rows = sb("masked_rows", [1, B])
        mask_scale = sb("mask_scale", [P, 2, NT])
        mask_bias = sb("mask_bias", [P, 2, NT])
        x_sb = sb("x_sb", [R2, PAIRS, H])
        normed = sb("normed", [R2, PAIRS, H])
        y = normed
        rowsT = sb("rowsT", [P, HALVES, ROWS])
        positive, negative = sb("positive", [R2, H]), sb("negative", [R2, H])
        stats, moments = sb("stats", [R2, PAIRS, 6]), sb("moments", [R2, PAIRS, 2])
        rstd = sb("rstd", [R2, PAIRS])
        delta = sb("delta", [R2, H])
        delta_stats, delta_moments, delta_rstd = sb("delta_stats", [R2, 6]), sb("delta_moments", [R2, 2]), sb("delta_rstd", [R2, 1])
        var_eps, newton = sb("var_eps", [R2, PAIRS]), sb("newton", [R2, PAIRS])
        fix, fix_neg, finite = sb("fix", [P, H]), sb("fix_neg", [P, H]), sb("finite", [P, H], U8)
        q_raw, q_high, q_rest = sb("q_raw", [P, HALVES, R2]), sb("q_high", [P, HALVES, R2], F32R), sb("q_rest", [P, HALVES, R2])
        q_rep = [sb(f"q_rep_{n}", [P, QG, R2]) for n in ("hi", "lo")]
        ctxT = [sb(f"ctxT{n}", [P, HALVES, CT]) for n in range(2 * CHUNKS)]
        ctx_hi = [sb(f"ctx_hi{c}", [P, HALVES, CT], F32R) for c in range(CHUNKS)]
        ctx_lo = [sb(f"ctx_lo{c}", [P, HALVES, CT], F32R) for c in range(CHUNKS)]
        k_split = sb("k_split", [P, QG, CT], F32R)
        ctx_sums, ctx_total = sb("ctx_sums", [P, HALVES, CHUNKS]), sb("ctx_total", [P, HALVES])
        unused = sb("unused", [P, HALVES, CT])
        v_masked, p_masked = sb("v_masked", [TT, NH, HD + 1]), sb("p_masked", [TT, S])
        zero_row = sb("zero_row", [1, ACC])
        masked_now = sb("masked_now", [1, 1])
        qbd = [[sb(f"qbd{b}_{n}", [P, QG, QH, S], F32R) for n in ("hi", "lo")] for b in range(2)]
        v = [sb(f"v{n}", [TT, NH, HD + 1]) for n in range(TPC)]
        p = [sb(f"p{n}", [TT, NH * S]) for n in range(TPC)]
        acc_sb, den_sb, inv_den = (sb(n, [P, ACC]) for n in ("acc_sb", "den_sb", "inv_den"))
        ctx_pair = sb("ctx_pair", [P, SLOTS, 2, S])
        logits, probs, weight = (sb(n, [R2, PAIRS, NE]) for n in ("logits", "probs", "weight"))
        above, ties = (sb(n, [R2, RPH, NE, NE]) for n in ("above", "ties"))
        row_max, row_sum, row_inv = (sb(n, [R2, RPH]) for n in ("row_max", "row_sum", "row_inv"))
        silu, act = sb("silu", [P, 2, HR]), sb("act", [P, 2, HR])

        bank = ctx.enter_context(nc.psum_tensor("bank", [P, 8, 512], F32))
        S_BANK = [0, 2]
        K_BANK = [2, 3]
        MISC_BANK = 5
        V_BANK = [4, 6]
        ACC_BANK = 7
        GU_BANK = [0, 2]
        D_BANK = [4, 6]
        acc = bank[:, ACC_BANK, 0:ACC]
        DEN_BANK = 0

        x_in = [sem(f"x_in{n}") for n in range(2)]
        mask_in, bias_in, small_in, late_in = (sem(n) for n in ("mask_in", "bias_in", "small_in", "late_in"))
        weights_ready, mask_made = sem("weights_ready"), sem("mask_made")
        wq_in, wk_in, wv_in, bv_in = (sem(n) for n in ("wq_in", "wk_in", "wv_in", "bv_in"))
        ctx_in = [sem(f"ctx_in{n}") for n in range(2 * CHUNKS)]
        ident_ready, consts = sem("ident_ready"), sem("consts")
        w_hi, w_lo = sem("w_hi"), sem("w_lo")
        chunk_high, chunk_low = sem("chunk_high"), sem("chunk_low")
        wo_clear, v_ones = sem("wo_clear"), sem("v_ones")
        any_ready, any_mm, general_ready, code_mm, counts_ready = (
            sem(n) for n in ("any_ready", "any_mm", "general_ready", "code_mm", "counts_ready"))
        sum_step, total_ready, v_sum_mm, v_masked_out = (
            sem(n) for n in ("sum_step", "total_ready", "v_sum_mm", "v_masked_out"))
        now_step = sem("now_step")
        batch_mm = sem("batch_mm")
        spare_clear = sem("spare_clear")
        chain = sem("chain")
        tanh_ready = sem("tanh_ready")
        x_moments, x_normal, x_parts, x_clean = (sem(n) for n in ("x_moments", "x_normal", "x_parts", "x_clean"))
        newton_step = sem("newton_step")
        misc_mm, misc_out = sem("misc_mm"), sem("misc_out")
        q_step, q_hi, q_lo, q_placed = (sem(n) for n in ("q_step", "q_hi", "q_lo", "q_placed"))
        mask_ready, qbd_ready = sem("mask_ready"), sem("qbd_ready")
        k_mm, k_hi, k_lo = sem("k_mm"), sem("k_hi"), sem("k_lo")
        v_mm, v_out = sem("v_mm"), sem("v_out")
        s_mm, exp_out, p_out = sem("s_mm"), sem("exp_out"), sem("p_out")
        pv_mm, acc_out, den_mm, den_out = sem("pv_mm"), sem("acc_out"), sem("den_mm"), sem("den_out")
        epi = sem("epi")
        delta_step, delta_scaled, x_updated = sem("delta_step"), sem("delta_scaled"), sem("x_updated")
        h_moments, h_normal = sem("h_moments"), sem("h_normal")
        shifted, e_out = sem("shifted"), sem("e_out")
        gu_mm, silu_out, act_out = sem("gu_mm"), sem("silu_out"), sem("act_out")
        d_mm, d_out = sem("d_mm"), sem("d_out")
        y_done, stored = sem("y_done"), sem("stored")

        def den_of(n):
            return bank[:, n, 256:256 + ACC]

        def read_code(engine, b):
            value = engine.value_load(code[0:1, bass.ds(b, 1)], min_val=0, max_val=CODE * (B * CHUNKS + 1))
            bits = [(value >> c) & 1 for c in range(CODE_BITS)]
            counts = [value >> CODE_BITS]
            for c in range(CHUNKS):
                counts.append(counts[-1] + bits[c])
            return bits, counts

        def build_qbd(engine, builder, b, parity, n, pair):
            after(engine, batch_mm, b - 1)
            engine.wait_ge(q_placed, 8 * pair + 4 * (n + 1))
            q = q_rep[n][:, :, S * parity:S * (parity + 1)].unsqueeze(2).broadcast_to([P, QG, QH, S])
            mask = head_mask[:].unsqueeze(1).unsqueeze(3).broadcast_to([P, QG, QH, S])
            builder.tensor_tensor(qbd[parity][n][:], q, mask, ALU.mult).then_inc(qbd_ready, 1)

        AHEAD = {0: (), 1: (0,), 2: (), 3: (1, 2), 4: (3, 4), 5: (5,)}

        X_TILES = [(0,), (1, 2), (3, 4), (5, 6), (7,)]
        H_TILES = [(0, 1), (2, 3), (4, 5), (6, 7)]

        def use_x(n):
            return n + 1 if n else 0

        def use_q(pair):
            return 2 * pair + 4 if not isinstance(pair, int) or pair else 1

        def use_o(pair):
            return 2 * pair + 7 if not isinstance(pair, int) or pair < PAIRS - 1 else USE_H[2] + 1

        USE_H = [2 * PAIRS + 4, 2 * PAIRS + 5, 2 * PAIRS + 7, 2 * PAIRS + 9]
        USE_R = [2 * PAIRS + 6, 2 * PAIRS + 10]
        def root_of(pair):
            return pair + 2 if not isinstance(pair, int) or pair < PAIRS - 1 else pair + 3

        H_ROOT = [PAIRS + 1, PAIRS + 3]
        CODE_BITS = 2 * CHUNKS
        CODE = 1 << CODE_BITS
        NEWTON = 7
        Q_STEPS, DELTA_STEPS = 5, 9

        block = ctx.enter_context(nc.Block())

        @block.sync
        def _(sp):
            x_rows = x_d.rearrange("(r p) h -> p r h", p=R2)
            sp.dma_start(x_sb[:, 0], x_rows[:, 0]).then_inc(x_in[0], 16)
            sp.dma_start(wq[:], wq_d).then_inc(wq_in, 16)
            sp.dma_start(x_sb[:, 1:PAIRS], x_rows[:, 1:PAIRS]).then_inc(x_in[1], 16)
            sp.dma_start(wk[:], wk_d).then_inc(wk_in, 16)
            sp.dma_start(wv[:], wv_d).then_inc(wv_in, 16)
            sp.dma_start(bv[:], bv_d.partition_broadcast(P)).then_inc(bv_in, 16)
            for c in range(CHUNKS):
                sp.dma_start(ctxT[c][:], ctx_d[0, c]).then_inc(ctx_in[c], 16)
            for c in range(CHUNKS):
                sp.dma_start(ctxT[CHUNKS + c][:], ctx_d[1, c]).then_inc(ctx_in[CHUNKS + c], 16)
            sp.wait_ge(wo_clear, 1)
            for j in range(GROUPS):
                sp.dma_start(wo[2 * HD * j:2 * HD * j + HD], wo_d[j]).then_inc(late_in, 16)
            for tile, source in ((bo, bo_d), (gamma, gamma_d), (beta, beta_d)):
                sp.dma_start(tile[:], source.partition_broadcast(P)).then_inc(late_in, 16)
            for tile, source in ((router, router_d), (gate_up, gate_up_d), (down, down_d)):
                sp.dma_start(tile[:], source).then_inc(late_in, 16)

            with sp.Fori(1, PAIRS) as pair:
                for odd in range(2):
                    for c in range(CHUNKS):
                        sp.wait_ge(chunk_high, (2 * pair + odd - 2) * CHUNKS + c + 1)
                        sp.wait_ge(chunk_low, (2 * pair + odd - 2) * CHUNKS + c + 1)
                        n = CHUNKS * odd + c
                        sp.dma_start(ctxT[n][:], ctx_d[2 * pair + odd, c]).then_inc(ctx_in[n], 16)
            out_rows = out_d.rearrange("(r p) h -> p r h", p=R2)
            for h in range(2):
                sp.wait_ge(y_done, h + 1)
                sp.dma_start(out_rows[:, RPH * h:RPH * (h + 1)], x_sb[:, RPH * h:RPH * (h + 1)]).then_inc(stored, 16)
            sp.wait_ge(stored, 32)
        LATE = 16 * (GROUPS + 6)

        @block.gpsimd
        def _(pool):
            pool.dma_start(mask_i[0:TT], mask_d).then_inc(mask_in, 16)
            for tile, source in ((bq, bq_d), (bk, bk_d)):
                pool.dma_start(tile[:], source).then_inc(bias_in, 16)
            nc.gpsimd.memset(ident[:], 0.0).then_inc(ident_ready, 1)
            nc.gpsimd.memset(eps[:], EPS_LN).then_inc(ident_ready, 1)
            nc.gpsimd.memset(minus_half[:], -0.5).then_inc(ident_ready, 1)
            nc.gpsimd.memset(three_halves[:], 1.5).then_inc(ident_ready, 1)
            pool.wait_ge(ident_ready, 4)
            nc.gpsimd.affine_select(out=ident[:], in_=ident[:], compare_op=ALU.not_equal, fill=1.0, base=0,
                                    pattern=[[-1, P]], channel_multiplier=1).then_inc(ident_ready, 1)

            def inverse_root(n, ready, count, var, root):
                w = var.shape[-1]
                v_e, t = var_eps[:, 0:w], newton[:, 0:w]
                pool.wait_ge(ready, count)
                after(pool, newton_step, NEWTON * n)
                steps = [(v_e, var, eps[:, 0:w], ALU.add), (root, v_e, minus_half[:, 0:w], ALU.pow),
                         (t, root, root, ALU.mult), (t, t, v_e, ALU.mult), (t, t, minus_half[:, 0:w], ALU.mult),
                         (t, t, three_halves[:, 0:w], ALU.add), (root, root, t, ALU.mult)]
                for k, (out, in0, in1, op) in enumerate(steps):
                    if k:
                        pool.wait_ge(newton_step, NEWTON * n + k)
                    nc.gpsimd.tensor_tensor(out, in0, in1, op).then_inc(newton_step, 1)

            inverse_root(0, x_moments, 1, moments[:, 0:1, 1], rstd[:, 0:1])
            nc.gpsimd.memset(code_weights[:], 1.0).then_inc(weights_ready, 1)
            w_code, w_own = code_weights[:, 0:B], code_weights[:, B:2 * B]
            pool.wait_ge(weights_ready, 1)
            nc.gpsimd.affine_select(out=w_code, in_=w_code, compare_op=ALU.is_ge, fill=0.0, base=-1,
                                    pattern=[[CHUNKS, B]], channel_multiplier=-1).then_inc(weights_ready, 1)
            pool.wait_ge(weights_ready, 2)
            nc.gpsimd.tensor_scalar(w_code, w_code, float(CODE), None, ALU.mult).then_inc(weights_ready, 1)
            for c in range(CODE_BITS):
                pool.wait_ge(weights_ready, 3 + c)
                nc.gpsimd.affine_select(out=w_code, in_=w_code, compare_op=ALU.not_equal, fill=float(1 << c), base=c,
                                        pattern=[[CHUNKS, B]], channel_multiplier=-1).then_inc(weights_ready, 1)
            pool.wait_ge(weights_ready, 3 + CODE_BITS)
            nc.gpsimd.affine_select(out=w_own, in_=w_own, compare_op=ALU.is_ge, fill=0.0, base=0,
                                    pattern=[[-CHUNKS, B]], channel_multiplier=1).then_inc(weights_ready, 1)
            pool.wait_ge(weights_ready, 4 + CODE_BITS)
            nc.gpsimd.affine_select(out=w_own, in_=w_own, compare_op=ALU.is_ge, fill=0.0, base=CHUNKS - 1,
                                    pattern=[[CHUNKS, B]], channel_multiplier=-1).then_inc(weights_ready, 1)
            nc.gpsimd.memset(head_of[:], 1.0).then_inc(consts, 1)
            pool.wait_ge(consts, 1)
            nc.gpsimd.affine_select(out=head_of[:], in_=head_of[:], compare_op=ALU.is_ge, fill=0.0, base=0,
                                    pattern=[[-HD, HH]], channel_multiplier=1).then_inc(consts, 1)
            pool.wait_ge(consts, 2)
            nc.gpsimd.affine_select(out=head_of[:], in_=head_of[:], compare_op=ALU.is_ge, fill=0.0, base=HD - 1,
                                    pattern=[[HD, HH]], channel_multiplier=-1).then_inc(consts, 1)
            pool.wait_ge(consts, 3)
            nc.gpsimd.tensor_tensor(head_mask[:], head_of[:, 0:QH], head_of[:, QH:HH], ALU.add).then_inc(mask_made, 1)
            inverse_root(1, x_moments, PAIRS, moments[:, 1:PAIRS, 1], rstd[:, 1:PAIRS])
            def delta_of(pair):
                inverse_root(root_of(pair), delta_step, DELTA_STEPS * pair + 8, delta_moments[:, 1:2], delta_rstd[:])
                pool.wait_ge(delta_step, DELTA_STEPS * pair + 9)
                nc.gpsimd.tensor_tensor(delta[:], delta[:], gamma[0:R2], ALU.mult).then_inc(delta_scaled, 1)
                pool.wait_ge(delta_scaled, 2 * pair + 1)
                nc.gpsimd.tensor_tensor(delta[:], delta[:], beta[0:R2], ALU.add).then_inc(delta_scaled, 1)

            for n, source in enumerate((gx_d, gf_d, rs_d)):
                pool.dma_start(gates[:, n:n + 1], source.partition_broadcast(P)).then_inc(small_in, 16)
            nc.gpsimd.memset(den_select[:], 0.0).then_inc(consts, 1)
            nc.gpsimd.memset(later_expert[:], 1.0).then_inc(consts, 1)
            nc.gpsimd.memset(wo[:], 0.0).then_inc(wo_clear, 1)
            pool.wait_ge(consts, 5)
            sel = den_select[:].rearrange("k (j m) -> k j m", j=GROUPS)
            nc.gpsimd.affine_select(out=sel, in_=sel, compare_op=ALU.not_equal, fill=1.0, base=-HD,
                                    pattern=[[-2 * HD, GROUPS], [0, 2 * HD]], channel_multiplier=1).then_inc(consts, 1)
            nc.gpsimd.affine_select(out=later_expert[:], in_=later_expert[:], compare_op=ALU.is_ge, fill=0.0,
                                    base=-1, pattern=[[1, NE], [-1, NE]], channel_multiplier=0).then_inc(consts, 1)

            for n in range(2):
                pool.wait_ge(qbd_ready, 2)
                build_qbd(pool, nc.gpsimd, 1, 1, n, 0)
            pool.wait_ge(late_in, LATE)
            with pool.Fori(0, PAIRS - 1) as pair:
                for n in range(2):
                    build_qbd(pool, nc.gpsimd, 2 * pair + 2, 0, n, pair + 1)
                for n in range(2):
                    build_qbd(pool, nc.gpsimd, 2 * pair + 3, 1, n, pair + 1)
                delta_of(pair)
            LAST = PAIRS - 1
            inverse_root(H_ROOT[0], h_moments, LAST, moments[:, 0:LAST, 1], rstd[:, 0:LAST])
            delta_of(LAST)
            inverse_root(H_ROOT[1], h_moments, PAIRS, moments[:, LAST:PAIRS, 1], rstd[:, LAST:PAIRS])
        CONSTS = 7
        SMALL = 16 * 3

        @block.tensor
        def _(pe):
            def transposes(tiles, use, ready, count):
                pe.wait_ge(ready, count)
                after(pe, misc_out, use)
                w = R2 * len(tiles)
                for k in range(HALVES):
                    for j, t in enumerate(tiles):
                        mm = nc.tensor.transpose(bank[:, MISC_BANK, w * k + R2 * j:w * k + R2 * (j + 1)],
                                                 normed[:, t, P * k:P * (k + 1)], ident[0:R2, 0:R2])
                mm.then_inc(misc_mm, 1)

            def x_transposes(n):
                transposes(X_TILES[n], use_x(n), x_clean, X_TILES[n][-1] + 1)

            def h_transposes(n):
                transposes(H_TILES[n], USE_H[n], h_normal, H_TILES[n][-1] + 1)

            def queries(pair):
                pe.wait_ge(misc_out, use_q(pair))
                for m in range(HALVES):
                    for k in range(HALVES):
                        mm = nc.tensor.matmul(bank[:, MISC_BANK, R2 * m:R2 * (m + 1)], wq[:, k, P * m:P * (m + 1)],
                                              rowsT[:, k, bass.ds(pair * R2, R2)],
                                              start=(k == 0), stop=(k == HALVES - 1))
                mm.then_inc(misc_mm, 1)

            def project_out(pair):
                pe.wait_ge(epi, 6 * pair + 6)
                pe.wait_ge(misc_out, use_o(pair))
                for slot in range(SLOTS):
                    mm = nc.tensor.matmul(bank[0:R2, MISC_BANK, 0:H], ctx_pair[:, slot].rearrange("p b s -> p (b s)"),
                                          wo[:, slot, :], start=(slot == 0), stop=(slot == SLOTS - 1))
                mm.then_inc(misc_mm, 1)

            def route(h):
                pe.wait_ge(misc_out, USE_R[h])
                for t in range(RPH):
                    r0 = HR * h + R2 * t
                    for k in range(HALVES):
                        mm = nc.tensor.matmul(bank[0:R2, MISC_BANK, NE * t:NE * (t + 1)], rowsT[:, k, r0:r0 + R2],
                                              router[:, k, :], start=(k == 0), stop=(k == HALVES - 1))
                mm.then_inc(misc_mm, 1)

            def find_general():
                pe.wait_ge(any_ready, 2)
                nc.tensor.matmul(bank[0:B * CHUNKS, 0, 0:1], chunk_any[0:TT], ones[0:TT], start=True,
                                 stop=True).then_inc(any_mm, 1)

            def encode():
                pe.wait_ge(weights_ready, 5 + CODE_BITS)
                pe.wait_ge(general_ready, 1)
                nc.tensor.matmul(bank[0:1, 1, 0:2 * B], general[:], code_weights[:], start=True,
                                 stop=True).then_inc(code_mm, 1)

            def k_proj(n, g):
                for m in range(HALVES):
                    terms = [(w, t, k) for w, t in ((wk_lo, ctx_hi), (wk_hi, ctx_lo), (wk_hi, ctx_hi))
                             for k in range(HALVES)]
                    for j, (w, t, k) in enumerate(terms):
                        mm = nc.tensor.matmul(bank[:, K_BANK[m], 0:CT], w[:, k, P * m:P * (m + 1)], t[n][:, k, :],
                                              start=(j == 0), stop=(j == len(terms) - 1))
                    mm.then_inc(k_mm, 1)

            def v_proj(n, t):
                t0 = TT * t
                terms = [(x, w, k) for x, w in ((ctx_lo, wv_hi), (ctx_hi, wv_lo), (ctx_hi, wv_hi)) for k in range(HALVES)]
                for j, (x, w, k) in enumerate(terms):
                    mm = nc.tensor.matmul(bank[0:TT, V_BANK[t], 0:H], x[n][:, k, t0:t0 + TT], w[:, k, :],
                                          start=(j == 0), stop=(j == len(terms) - 1))
                mm.then_inc(v_mm, 1)

            def scores(parity, t):
                for g in range(QG):
                    col = QW * (g % 2)
                    for n in range(2):
                        mm = nc.tensor.matmul(bank[0:TT, S_BANK[t] + g // 2, col:col + QW],
                                              k_split[:, g, TT * t:TT * (t + 1)], qbd[parity][n][:, g],
                                              start=(n == 0), stop=(n == 1))
                mm.then_inc(s_mm, 1)

            def p_v(v_rows, p_rows, p_heads, semaphore):
                for slot in range(SLOTS):
                    for j in range(GROUPS):
                        h = GROUPS * slot + j
                        p_cols = p_rows[:, S * h:S * (h + 1)] if p_heads else p_rows
                        mm = nc.tensor.matmul(acc[2 * HD * j:2 * HD * j + HD + 1, S * slot:S * (slot + 1)],
                                              v_rows[:, h, 0:HD + 1], p_cols, start=False, stop=False,
                                              skip_group_check=True)
                mm.then_inc(semaphore, 1)

            def attend_chunk(b, parity, c, g):
                pe.wait_ge(chunk_low, CHUNKS * b + c + 1)
                k_proj(c, g)
                v_proj(c, 0)
                pe.wait_ge(qbd_ready, 2 * (b + 1))
                pe.wait_ge(k_lo, QG * (g + 1))
                after(pe, den_out, b)
                scores(parity, 0)
                pe.wait_ge(v_masked_out, b + 1)
                v_proj(c, 1)
                scores(parity, 1)
                for t in range(TPC):
                    pe.wait_ge(v_out, TPC * g + t + 1)
                    pe.wait_ge(p_out, TPC * g + t + 1)
                    p_v(v[t], p[t], True, pv_mm)

            def sum_v_of_masked(b):
                pe.wait_ge(total_ready, b + 1)
                for k in range(HALVES):
                    mm = nc.tensor.matmul(bank[0:1, V_BANK[1], 0:H], ctx_total[:, k:k + 1], wv[:, k, :],
                                          start=(k == 0), stop=(k == HALVES - 1))
                mm.then_inc(v_sum_mm, 1)

            def masked_chunks(b):
                pe.wait_ge(v_masked_out, b + 1)
                p_v(v_masked, p_masked[:], False, batch_mm)

            def denominators(b, den_bank):
                pe.wait_ge(acc_out, b + 1)
                nc.tensor.matmul(den_of(den_bank), den_select[:], acc_sb[:], start=True, stop=True,
                                 skip_group_check=True).then_inc(den_mm, 1)

            def batch(b, parity, work, first=False, last=False):
                bits, g = read_code(pe, b)
                if not first:
                    denominators(b - 1, DEN_BANK)
                nc.tensor.matmul(acc, zero_row[0:1, 0:P], zero_row[:], start=True, stop=False, skip_group_check=True)
                for c in range(CHUNKS):
                    with pe.If(bits[c] > 0):
                        attend_chunk(b, parity, c, g[c])
                    work(c)
                masked_chunks(b)
                if not last:
                    sum_v_of_masked(b + 1)

            def first_work(c):
                for n in {1: (1,), 2: (2,), 3: (3, 4)}.get(c, ()):
                    x_transposes(n)

            def odd_work(pair, c):
                if c == 0:
                    queries(pair + 1)

            def even_work(pair, c):
                if c == 2:
                    project_out(pair)

            def last_work(c):
                if c == 5:
                    h_transposes(0)
                    h_transposes(1)
                    route(0)
                    h_transposes(2)

            find_general()
            pe.wait_ge(ident_ready, 5)
            x_transposes(0)
            pe.wait_ge(wq_in, 16)
            queries(0)
            encode()
            pe.wait_ge(w_hi, 2)
            pe.wait_ge(w_lo, 2)
            pe.wait_ge(consts, CONSTS)
            pe.wait_ge(v_ones, TPC + 3)
            pe.wait_ge(counts_ready, 2)
            sum_v_of_masked(0)
            batch(0, 0, first_work, first=True)
            pe.wait_ge(late_in, LATE)
            with pe.Fori(0, PAIRS - 1) as pair:
                batch(2 * pair + 1, 1, lambda c: odd_work(pair, c))
                batch(2 * pair + 2, 0, lambda c: even_work(pair, c))
            batch(B - 1, 1, last_work, last=True)

            def expert_in(s):
                h, e = s // NE, s % NE
                after(pe, act_out, s - 1)
                for g in range(2):
                    for k in range(HALVES):
                        mm = nc.tensor.matmul(bank[:, GU_BANK[s % 2] + g, 0:HR], gate_up[:, e, k, g, :],
                                              rowsT[:, k, HR * h:HR * (h + 1)],
                                              start=(k == 0), stop=(k == HALVES - 1))
                mm.then_inc(gu_mm, 1)

            def expert_out(s):
                e = s % NE
                pe.wait_ge(act_out, s + 1)
                for n in range(2):
                    after(pe, d_out, RPH * (s - 1) + 2 * (n + 1))
                    for k in range(2):
                        t = 2 * n + k
                        mm = nc.tensor.matmul(bank[0:R2, D_BANK[n], H * k:H * (k + 1)],
                                              act[:, s % 2, R2 * t:R2 * (t + 1)], down[:, e, :], start=True, stop=True)
                    mm.then_inc(d_mm, 1)

            pe.wait_ge(misc_out, USE_H[1] + 1)
            expert_in(0)
            denominators(B - 1, ACC_BANK)
            for s in range(2 * NE):
                if s + 1 == NE:
                    pe.wait_ge(misc_out, USE_H[3] + 1)
                if s + 1 < 2 * NE:
                    expert_in(s + 1)
                if s == 0:
                    project_out(PAIRS - 1)
                if s == 4:
                    h_transposes(3)
                if s == 5:
                    route(1)
                expert_out(s)

        @block.scalar
        def _(act_e):
            def k_high(g):
                for m in range(HALVES):
                    act_e.wait_ge(k_mm, HALVES * g + m + 1)
                    for a in range(2):
                        n = 2 * m + a
                        nc.scalar.activation(k_split[0:64, n, :], bank[64 * a:64 * (a + 1), K_BANK[m], 0:CT],
                                             ACT.Identity, bias=bk[:, n:n + 1]).then_inc(k_hi, 1)

            def read_chunk(b, turn, parity, c, general, done):
                n = CHUNKS * parity + c
                with act_e.If(general > 0):
                    act_e.wait_ge(ctx_in[n], 16 * turn + 16)
                    act_e.wait_ge(v_mm, 1 + TPC * done)
                    nc.scalar.copy(ctx_hi[c][:], ctxT[n][:]).then_inc(chunk_high, 1)
                with act_e.Else():
                    act_e.wait_ge(ctx_in[n], 16 * turn + 16)
                    after(act_e, total_ready, b)
                    after(act_e, chunk_high, CHUNKS * b + c)
                    for k in range(HALVES):
                        ins = nc.scalar.activation(unused[:, k], ctxT[n][:, k], ACT.Identity,
                                                   accum_out=ctx_sums[:, k, c:c + 1])
                    ins.then_inc(chunk_high, 1)

            def exps(parity, c, g):
                for t in range(TPC):
                    i = TPC * c + t
                    act_e.wait_ge(s_mm, TPC * g + t + 1)
                    banks = bank[0:TT, S_BANK[t]:S_BANK[t] + HALVES, 0:HALF]
                    nc.scalar.activation(p[t][:].rearrange("t (m n) -> t m n", m=HALVES), banks, ACT.Exp,
                                         bias=mask_bias[0:TT, parity, i:i + 1],
                                         scale=mask_scale[0:TT, parity, i:i + 1]).then_inc(exp_out, 1)

            def copy_transposes(tiles, use):
                act_e.wait_ge(misc_mm, use + 1)
                w = R2 * len(tiles)
                nc.scalar.copy(rowsT[:, :, R2 * tiles[0]:R2 * tiles[0] + w],
                               bank[:, MISC_BANK, 0:HALVES * w].rearrange("p (k n) -> p k n", k=HALVES)
                               ).then_inc(misc_out, 1)

            def q_bias(pair):
                act_e.wait_ge(misc_mm, use_q(pair) + 1)
                for m in range(HALVES):
                    ins = nc.scalar.activation(q_raw[:, m], bank[:, MISC_BANK, R2 * m:R2 * (m + 1)], ACT.Identity,
                                               bias=bq[:, m:m + 1])
                ins.then_inc(misc_out, 1)

            def q_highs(pair):
                act_e.wait_ge(q_step, Q_STEPS * (pair + 1))
                nc.scalar.copy(q_high[:], fix[:, 0:HALVES * R2].rearrange("p (m r) -> p m r", m=HALVES)).then_inc(q_hi, 1)

            def place_queries(pair, n):
                act_e.wait_ge(q_lo, pair + 1)
                after(act_e, qbd_ready, 4 * pair)
                source = q_high[:].bitcast(F32) if n == 0 else q_rest[:]
                for a in range(2):
                    for copy in range(2):
                        out = q_rep[n][64 * copy:64 * (copy + 1)].rearrange("p (m a) r -> p m a r", a=2)[:, :, a]
                        nc.scalar.copy(out, source[64 * a:64 * (a + 1)]).then_inc(q_placed, 1)

            def acc_copy(b):
                act_e.wait_ge(batch_mm, b + 1)
                nc.scalar.copy(acc_sb[:], acc).then_inc(acc_out, 1)

            def den_copy(b, den_bank):
                act_e.wait_ge(den_mm, b + 1)
                nc.scalar.copy(den_sb[:], den_of(den_bank)).then_inc(den_out, 1)

            def batch(b, parity, turn, work, first=False, last=False):
                bits, g = read_code(act_e, b)
                if not first:
                    acc_copy(b - 1)
                    den_copy(b - 1, DEN_BANK)
                for c in range(CHUNKS):
                    with act_e.If(bits[c] > 0):
                        k_high(g[c])
                        act_e.wait_ge(mask_ready, b + 1)
                        exps(parity, c, g[c])
                    for r in () if last else AHEAD[c]:
                        read_chunk(b + 1, turn + parity, 1 - parity, r, bits[CHUNKS + r], g[r + 1])
                    work(c)

            def first_work(c):
                for n in {1: (1,), 2: (2,), 3: (3, 4)}.get(c, ()):
                    copy_transposes(X_TILES[n], use_x(n))

            def odd_work(pair, c):
                if c == 0:
                    q_bias(pair + 1)
                if c == 5:
                    q_highs(pair + 1)
                    place_queries(pair + 1, 0)
                    place_queries(pair + 1, 1)

            def last_work(c):
                if c == 5:
                    for n in range(2):
                        copy_transposes(H_TILES[n], USE_H[n])
                    exps_of_logits(0)
                    copy_transposes(H_TILES[2], USE_H[2])

            def exps_of_logits(h):
                act_e.wait_ge(shifted, h + 1)
                nc.scalar.activation(probs[:, RPH * h:RPH * (h + 1)], logits[:, RPH * h:RPH * (h + 1)],
                                     ACT.Exp).then_inc(e_out, 1)

            copy_transposes(X_TILES[0], use_x(0))
            act_e.wait_ge(bias_in, 32)
            q_bias(0)
            act_e.wait_ge(wk_in, 16)
            nc.scalar.copy(wk_hi[:], wk[:]).then_inc(w_hi, 1)
            act_e.wait_ge(wv_in, 16)
            nc.scalar.copy(wv_hi[:], wv[:]).then_inc(w_hi, 1)
            q_highs(0)
            place_queries(0, 0)
            place_queries(0, 1)
            act_e.wait_ge(counts_ready, 2)
            bits, _ = read_code(act_e, 0)
            for c in range(CHUNKS):
                read_chunk(0, 0, 0, c, bits[c], 0)
            act_e.wait_ge(small_in, SMALL)
            nc.scalar.activation(tanhs[:], gates[:, 0:2], ACT.Tanh).then_inc(tanh_ready, 1)
            batch(0, 0, 0, first_work, first=True)
            with act_e.Fori(0, PAIRS - 1) as pair:
                batch(2 * pair + 1, 1, pair, lambda c: odd_work(pair, c))
                batch(2 * pair + 2, 0, pair + 1, lambda c: None)
            batch(B - 1, 1, PAIRS - 1, last_work, last=True)

            acc_copy(B - 1)
            den_copy(B - 1, ACC_BANK)
            for s in range(2 * NE):
                act_e.wait_ge(gu_mm, s + 1)
                after(act_e, act_out, s - 1)
                nc.scalar.activation(silu[:, s % 2], bank[:, GU_BANK[s % 2], 0:HR], ACT.Silu).then_inc(silu_out, 1)
                if s == 5:
                    copy_transposes(H_TILES[3], USE_H[3])
                if s == 6:
                    exps_of_logits(1)

        @block.vector
        def _(dve):
            count = [0]

            def step(ins):
                count[0] += 1
                ins.then_inc(chain, 1)
                dve.wait_ge(chain, count[0])

            def stand_still(semaphore, count):
                dve.wait_ge(semaphore, count)
                nc.vector.tensor_copy(spare[:, 0:1], spare[:, 1:2])

            def clean(t, f, g, m, semaphore, done, part):
                if part == 0:
                    nc.vector.tensor_scalar(f, t, 0.0, LIM, ALU.max, ALU.min).then_inc(semaphore, 1)
                    nc.vector.tensor_scalar(g, t, 0.0, -LIM, ALU.min, ALU.max).then_inc(semaphore, 1)
                    nc.vector.tensor_scalar(m, t, 0.0, 0.0, ALU.mult, ALU.is_equal).then_inc(semaphore, 1)
                if part == 1:
                    dve.wait_ge(semaphore, done + 2)
                    nc.vector.tensor_tensor(f, f, g, ALU.add).then_inc(semaphore, 1)
                    stand_still(semaphore, done + 4)
                    nc.vector.copy_predicated(f, m, t).then_inc(semaphore, 1)

            def moments_of(tiles, ready):
                for t in tiles:
                    ins = nc.vector.bn_stats(stats[:, t, :], x_sb[:, t])
                step(ins)
                for t in tiles:
                    nc.vector.bn_aggr(moments[:, t, :], stats[:, t, :]).then_inc(ready, 1)

            def normalise_rows(t, root, ready):
                dve.wait_ge(newton_step, NEWTON * (root + 1))
                nc.vector.tensor_scalar(normed[:, t], x_sb[:, t], moments[:, t, 0:1], rstd[:, t:t + 1],
                                        ALU.subtract, ALU.mult).then_inc(ready, 1)

            def rest_of_chunk(b, parity, c, general, done):
                n = CHUNKS * parity + c
                with dve.If(general > 0):
                    dve.wait_ge(chunk_high, CHUNKS * b + c + 1)
                    dve.wait_ge(v_mm, 1 + TPC * done)
                    after(dve, total_ready, b)
                    nc.vector.memset(ctx_sums[:, :, c:c + 1], 0.0).then_inc(sum_step, 1)
                    nc.vector.tensor_tensor(ctx_lo[c][:], ctxT[n][:], ctx_hi[c][:].bitcast(F32),
                                            ALU.subtract).then_inc(chunk_low, 1)
                with dve.Else():
                    nc.vector.tensor_copy(passed[:, c:c + 1], spare[:, 1:2]).then_inc(chunk_low, 1)

            def k_low(g):
                for m in range(HALVES):
                    for a in range(2):
                        n = 2 * m + a
                        dve.wait_ge(k_hi, QG * g + n + 1)
                        nc.vector.scalar_tensor_tensor(k_split[64:128, n, :], bank[64 * a:64 * (a + 1), K_BANK[m], 0:CT],
                                                       bk[:, n:n + 1], k_split[0:64, n, :].bitcast(F32),
                                                       ALU.add, ALU.subtract).then_inc(k_lo, 1)

            def clean_queries(pair, part):
                dve.wait_ge(misc_out, use_q(pair) + 1)
                w = HALVES * R2
                clean(q_raw[:].rearrange("p m r -> p (m r)"), fix[:, 0:w], fix_neg[:, 0:w], finite[:, 0:w],
                      q_step, Q_STEPS * pair, part)

            def low_queries(pair):
                dve.wait_ge(q_hi, pair + 1)
                nc.vector.tensor_tensor(q_rest[:], fix[:, 0:HALVES * R2].rearrange("p (m r) -> p m r", m=HALVES),
                                        q_high[:].bitcast(F32), ALU.subtract).then_inc(q_lo, 1)

            def mask_of(b, parity):
                after(dve, acc_out, b - 1)
                cols = attend[0:TT, bass.ds(b * NT, NT)]
                nc.vector.tensor_scalar(mask_scale[0:TT, parity], cols, HD ** -0.5, None, ALU.mult)
                nc.vector.tensor_scalar(mask_bias[0:TT, parity], cols, 1.0, CLIP, ALU.subtract,
                                        ALU.mult).then_inc(mask_ready, 1)

            def v_copy(g, t):
                dve.wait_ge(v_mm, 1 + TPC * g + t + 1)
                nc.vector.tensor_tensor(v[t][:, :, 0:HD],
                                        bank[0:TT, V_BANK[t], 0:H].rearrange("t (h d) -> t h d", h=NH),
                                        bv[0:TT].rearrange("t (h d) -> t h d", h=NH), ALU.add).then_inc(v_out, 1)

            def p_clip(g, t):
                dve.wait_ge(exp_out, TPC * g + t + 1)
                nc.vector.tensor_scalar(p[t][:], p[t][:], E_HI, E_LO, ALU.min, ALU.max).then_inc(p_out, 1)

            def total_of_masked(b):
                dve.wait_ge(chunk_high, CHUNKS * (b + 1))
                dve.wait_ge(chunk_low, CHUNKS * (b + 1))
                after(dve, v_sum_mm, b)
                nc.vector.tensor_reduce(ctx_total[:], ctx_sums[:], AX_X, ALU.add).then_inc(total_ready, 1)

            def v_of_masked(b):
                dve.wait_ge(v_sum_mm, b + 1)
                rows = masked_rows[0:1, bass.ds(b, 1)]
                after(dve, batch_mm, b)
                nc.vector.tensor_copy(v_masked[0:1, :, HD:HD + 1], rows.unsqueeze(1).broadcast_to([1, NH, 1]))
                nc.vector.tensor_copy(masked_now[:], rows).then_inc(now_step, 1)
                dve.wait_ge(now_step, b + 1)
                nc.vector.scalar_tensor_tensor(v_masked[0:1, :, 0:HD], bv[0:1].rearrange("t (h d) -> t h d", h=NH),
                                               masked_now[:], bank[0:1, V_BANK[1], 0:H].rearrange("t (h d) -> t h d", h=NH),
                                               ALU.mult, ALU.add).then_inc(v_masked_out, 1)

            def normalise(b, parity, part):
                dve.wait_ge(den_out, b + 1)
                if part == 0:
                    nc.vector.scalar_tensor_tensor(inv_den[:], den_sb[:], 1e-8, den_sb[:], ALU.mult,
                                                   ALU.add).then_inc(epi, 1)
                if part == 1:
                    dve.wait_ge(epi, 3 * b + 1)
                    nc.vector.reciprocal(inv_den[:], inv_den[:]).then_inc(epi, 1)
                if part == 2:
                    dve.wait_ge(epi, 3 * b + 2)
                    nc.vector.tensor_tensor(ctx_pair[:, :, parity],
                                            acc_sb[:].rearrange("p (r s) -> p r s", r=SLOTS),
                                            inv_den[:].rearrange("p (r s) -> p r s", r=SLOTS),
                                            ALU.mult).then_inc(epi, 1)

            def delta_clean(pair, part):
                if part == 0:
                    dve.wait_ge(misc_mm, use_o(pair) + 1)
                    nc.vector.tensor_tensor(delta[:], bank[0:R2, MISC_BANK, 0:H], bo[0:R2], ALU.add).then_inc(misc_out, 1)
                    dve.wait_ge(misc_out, use_o(pair) + 1)
                clean(delta[:], fix[0:R2], fix_neg[0:R2], finite[0:R2], delta_step, DELTA_STEPS * pair, part)

            def delta_moments_of(pair):
                done = DELTA_STEPS * pair
                dve.wait_ge(delta_step, done + 5)
                nc.vector.tensor_scalar(delta[:], fix[0:R2], rscale[0:R2], None, ALU.mult).then_inc(delta_step, 1)
                dve.wait_ge(delta_step, done + 6)
                nc.vector.bn_stats(delta_stats[:], delta[:]).then_inc(delta_step, 1)
                stand_still(delta_step, done + 7)
                nc.vector.bn_aggr(delta_moments[:], delta_stats[:]).then_inc(delta_step, 1)

            def delta_normalise(pair):
                dve.wait_ge(newton_step, NEWTON * (root_of(pair) + 1))
                nc.vector.tensor_scalar(delta[:], delta[:], delta_moments[:, 0:1], delta_rstd[:],
                                        ALU.subtract, ALU.mult).then_inc(delta_step, 1)

            def add_delta(pair):
                dve.wait_ge(delta_scaled, 2 * pair + 2)
                x_tile = x_sb[:, bass.ds(pair, 1)].rearrange("p a h -> p (a h)")
                nc.vector.scalar_tensor_tensor(x_tile, delta[:], tanhs[0:R2, 0:1], x_tile,
                                               ALU.mult, ALU.add).then_inc(x_updated, 1)

            def shift_logits(h):
                half = logits[:, RPH * h:RPH * (h + 1)]
                dve.wait_ge(misc_mm, USE_R[h] + 1)
                nc.vector.tensor_copy(half, bank[0:R2, MISC_BANK, 0:RPH * NE].rearrange("p (r e) -> p r e", r=RPH)
                                      ).then_inc(misc_out, 1)
                dve.wait_ge(misc_out, USE_R[h] + 1)
                step(nc.vector.tensor_reduce(row_max[:], half, AX_X, ALU.max))
                nc.vector.tensor_tensor(half, half, row_max[:].unsqueeze(2).broadcast_to([R2, RPH, NE]),
                                        ALU.subtract).then_inc(shifted, 1)

            def expert_ranks(h):
                by_row = [R2, RPH, NE]
                pr, wt = probs[:, RPH * h:RPH * (h + 1)], weight[:, RPH * h:RPH * (h + 1)]
                dve.wait_ge(e_out, h + 1)
                step(nc.vector.tensor_reduce(row_sum[:], pr, AX_X, ALU.add))
                step(nc.vector.reciprocal(row_inv[:], row_sum[:]))
                step(nc.vector.tensor_tensor(pr, pr, row_inv[:].unsqueeze(2).broadcast_to(by_row), ALU.mult))
                pairs = [R2, RPH, NE, NE]
                mine, other = pr.unsqueeze(3).broadcast_to(pairs), pr.unsqueeze(2).broadcast_to(pairs)
                step(nc.vector.tensor_tensor(above[:], other, mine, ALU.is_gt))
                step(nc.vector.tensor_tensor(ties[:], other, mine, ALU.is_equal))
                step(nc.vector.tensor_tensor(ties[:], ties[:], later_expert[0:R2].unsqueeze(1).broadcast_to(pairs),
                                             ALU.mult))
                step(nc.vector.tensor_tensor(above[:], above[:], ties[:], ALU.add))

            def expert_weights(h):
                by_row = [R2, RPH, NE]
                pr, wt = probs[:, RPH * h:RPH * (h + 1)], weight[:, RPH * h:RPH * (h + 1)]
                step(nc.vector.tensor_reduce(wt, above[:], AX_X, ALU.add))
                step(nc.vector.tensor_scalar(wt, wt, 1.5, None, ALU.is_lt))
                step(nc.vector.tensor_tensor(wt, wt, pr, ALU.mult))
                step(nc.vector.tensor_reduce(row_sum[:], wt, AX_X, ALU.add))
                step(nc.vector.reciprocal(row_inv[:], row_sum[:]))
                step(nc.vector.tensor_tensor(wt, wt, row_inv[:].unsqueeze(2).broadcast_to(by_row), ALU.mult))

            def batch(b, parity, work, first=False, last=False):
                bits, g = read_code(dve, b)
                for c in range(CHUNKS):
                    if c == 0:
                        v_of_masked(b)
                    with dve.If(bits[c] > 0):
                        k_low(g[c])
                        v_copy(g[c], 0)
                        v_copy(g[c], 1)
                        p_clip(g[c], 0)
                        p_clip(g[c], 1)
                    for r in () if last else AHEAD[c]:
                        rest_of_chunk(b + 1, 1 - parity, r, bits[CHUNKS + r], g[r + 1])
                    if c == CHUNKS - 1 and not last:
                        total_of_masked(b + 1)
                    if c == 0 and not last:
                        mask_of(b + 1, 1 - parity)
                    if c == 1 and not first:
                        for part in range(3):
                            normalise(b - 1, 1 - parity, part)
                    work(c)

            def clean_rows(t):
                dve.wait_ge(x_normal, t + 1)
                step(nc.vector.tensor_scalar(fix[0:R2], normed[:, t], 0.0, None, ALU.max))
                nc.vector.scalar_tensor_tensor(normed[:, t], normed[:, t], 0.0, fix[0:R2], ALU.min,
                                               ALU.add).then_inc(x_clean, 1)

            def first_work(c):
                for t in {0: (1, 2), 1: (3, 4), 2: (5, 6, 7)}.get(c, ()):
                    normalise_rows(t, 1, x_normal)
                    clean_rows(t)
            def odd_work(pair, c):
                if c == 4:
                    clean_queries(pair + 1, 0)
                    clean_queries(pair + 1, 1)
                if c == 5:
                    low_queries(pair + 1)
            def even_work(pair, c):
                if c == 3:
                    delta_clean(pair, 0)
                    delta_clean(pair, 1)
                    delta_moments_of(pair)
                if c == 4:
                    delta_normalise(pair)
                if c == 5:
                    add_delta(pair)

            def last_work(c):
                if c in (0, 1):
                    moments_of(range(RPH) if c == 0 else range(RPH, PAIRS - 1), h_moments)
                if c == 5:
                    for t in range(PAIRS - 1):
                        normalise_rows(t, H_ROOT[0], h_normal)
                    shift_logits(0)

            nc.vector.memset(spare[:], 0.0).then_inc(spare_clear, 1)
            dve.wait_ge(spare_clear, 1)
            nc.vector.memset(ones[:], 1.0).then_inc(any_ready, 1)
            nc.vector.memset(zero_row[:], 0.0).then_inc(v_ones, 1)
            nc.vector.memset(v_masked[:], 0.0).then_inc(v_ones, 1)
            nc.vector.memset(p_masked[:], E_LO).then_inc(v_ones, 1)
            nc.vector.memset(masked_now[:], 0.0).then_inc(v_mm, 1)
            for n in range(TPC):
                nc.vector.memset(v[n][:], 1.0).then_inc(v_ones, 1)
            dve.wait_ge(mask_in, 16)
            step(nc.vector.tensor_copy(attend[0:TT], mask_i[0:TT]))
            step(nc.vector.tensor_scalar(attend[0:TT], attend[0:TT], 0.5, None, ALU.is_gt))
            nc.vector.tensor_reduce(chunk_any[0:TT], attend[0:TT].rearrange("t (n i) -> t n i", i=TPC), AX_X,
                                    ALU.max).then_inc(any_ready, 1)
            dve.wait_ge(any_mm, 1)
            nc.vector.tensor_scalar(general[:], bank[0:B * CHUNKS, 0, 0:1], 0.5, None, ALU.is_gt).then_inc(general_ready, 1)
            dve.wait_ge(x_in[0], 16)
            moments_of((0,), x_moments)
            normalise_rows(0, 0, x_normal)
            clean_rows(0)
            dve.wait_ge(x_in[1], 16)
            moments_of(range(1, PAIRS), x_moments)
            dve.wait_ge(w_hi, 1)
            nc.vector.tensor_tensor(wk_lo[:], wk[:], wk_hi[:].bitcast(F32), ALU.subtract).then_inc(w_lo, 1)
            dve.wait_ge(bias_in, 32)
            clean_queries(0, 0)
            clean_queries(0, 1)
            low_queries(0)
            dve.wait_ge(code_mm, 1)
            step(nc.vector.tensor_copy(code_f[:], bank[0:1, 1, 0:2 * B]))
            nc.vector.tensor_copy(code[:], code_f[:, 0:B]).then_inc(counts_ready, 1)
            nc.vector.tensor_scalar(masked_rows[:], code_f[:, B:2 * B], -float(CT), float(T), ALU.mult,
                                    ALU.add).then_inc(counts_ready, 1)
            dve.wait_ge(w_hi, 2)
            nc.vector.tensor_tensor(wv_lo[:], wv[:], wv_hi[:].bitcast(F32), ALU.subtract).then_inc(w_lo, 1)
            dve.wait_ge(mask_made, 1)
            build_qbd(dve, nc.vector, 0, 0, 0, 0)
            build_qbd(dve, nc.vector, 0, 0, 1, 0)
            mask_of(0, 0)
            dve.wait_ge(small_in, SMALL)
            step(nc.vector.tensor_scalar(rscale[:], gates[:, 2:3], 0.0, 0.3, ALU.max, ALU.min))
            dve.wait_ge(bv_in, 16)
            dve.wait_ge(counts_ready, 2)
            bits, _ = read_code(dve, 0)
            for c in range(CHUNKS):
                rest_of_chunk(0, 0, c, bits[c], 0)
            total_of_masked(0)
            batch(0, 0, first_work, first=True)
            dve.wait_ge(late_in, LATE)
            dve.wait_ge(tanh_ready, 1)
            with dve.Fori(0, PAIRS - 1) as pair:
                batch(2 * pair + 1, 1, lambda c: odd_work(pair, c))
                batch(2 * pair + 2, 0, lambda c: even_work(pair, c))
            dve.wait_ge(x_updated, PAIRS - 1)
            batch(B - 1, 1, last_work, last=True)
            expert_ranks(0)
            for part in range(3):
                normalise(B - 1, 1, part)

            def gate(s):
                dve.wait_ge(silu_out, s + 1)
                after(dve, d_mm, 2 * (s - 1))
                nc.vector.tensor_tensor(act[:, s % 2], silu[:, s % 2], bank[:, GU_BANK[s % 2] + 1, 0:HR],
                                        ALU.mult).then_inc(act_out, 1)

            def add_expert(s):
                for t in range(RPH):
                    n, r, e = RPH * s + t, RPH * (s // NE) + t, s % NE
                    dve.wait_ge(d_mm, n // 2 + 1)
                    out, share = bank[0:R2, D_BANK[t // 2], H * (t % 2):H * (t % 2 + 1)], weight[:, r, e:e + 1]
                    if e == 0:
                        nc.vector.tensor_scalar(y[:, r], out, share, None, ALU.mult).then_inc(d_out, 1)
                    else:
                        dve.wait_ge(d_out, n - RPH + 1)
                        nc.vector.scalar_tensor_tensor(y[:, r], out, share, y[:, r], ALU.mult, ALU.add).then_inc(d_out, 1)

            def finish(h):
                dve.wait_ge(d_out, ROWS // R2 * NE // 2 * (h + 1))
                half = x_sb[:, RPH * h:RPH * (h + 1)].rearrange("p r h -> p (r h)")
                nc.vector.scalar_tensor_tensor(half, y[:, RPH * h:RPH * (h + 1)].rearrange("p r h -> p (r h)"),
                                               tanhs[0:R2, 1:2], half, ALU.mult, ALU.add).then_inc(y_done, 1)

            gate(0)
            expert_weights(0)
            for s in range(2 * NE):
                if s + 1 < 2 * NE:
                    gate(s + 1)
                if s == 0:
                    delta_clean(PAIRS - 1, 0)
                add_expert(s)
                if s == 0:
                    delta_clean(PAIRS - 1, 1)
                    delta_moments_of(PAIRS - 1)
                if s == 1:
                    delta_normalise(PAIRS - 1)
                if s == 2:
                    add_delta(PAIRS - 1)
                    dve.wait_ge(x_updated, PAIRS)
                    moments_of((PAIRS - 1,), h_moments)
                if s == 3:
                    normalise_rows(PAIRS - 1, H_ROOT[1], h_normal)
                if s == 5:
                    shift_logits(1)
                if s == 6:
                    expert_ranks(1)
                if s == NE - 1:
                    expert_weights(1)
                    finish(0)
            finish(1)


def kernel(x, ctx_2048, mask_BxS2_ik0, g_xattn, g_ffn, L0_xattn_Wq, L0_xattn_bq, L0_xattn_Wk, L0_xattn_bk,
           L0_xattn_Wv, L0_xattn_bv, L0_xattn_Wo, L0_xattn_bo, L0_xattn_ln_gamma, L0_xattn_ln_beta,
           L0_xattn_residual_scale, L0_ffn_router_gate, L0_ffn_expert_gate_up, L0_ffn_expert_down):
    import concourse.bacc as bacc
    from concourse.bass_utils import run_bass_kernel_spmd

    def rows_by_block(w):
        return np.asarray(w).T.reshape(HALVES, P, -1).transpose(1, 0, 2)

    ctx_l = np.asarray(ctx_2048).reshape(B, CHUNKS, CT, HALVES, P).transpose(0, 1, 4, 3, 2)
    mask_l = np.asarray(mask_BxS2_ik0).reshape(B * NT, TT).T
    wo_l = np.asarray(L0_xattn_Wo).T.reshape(SLOTS, GROUPS, HD, H).transpose(1, 2, 0, 3)
    gu_l = np.asarray(L0_ffn_expert_gate_up).reshape(NE, HALVES, P, FF, 2).transpose(2, 0, 1, 4, 3)
    arrays = {
        "x": np.asarray(x).reshape(ROWS, H), "ctx": ctx_l, "mask": mask_l,
        "gx": np.asarray(g_xattn), "gf": np.asarray(g_ffn),
        "wq": rows_by_block(L0_xattn_Wq), "bq": np.asarray(L0_xattn_bq).reshape(HALVES, P).T,
        "wk": rows_by_block(L0_xattn_Wk), "bk": np.asarray(L0_xattn_bk).reshape(QG, P // 2).T,
        "wv": rows_by_block(L0_xattn_Wv), "bv": np.asarray(L0_xattn_bv),
        "wo": wo_l, "bo": np.asarray(L0_xattn_bo),
        "gamma": np.asarray(L0_xattn_ln_gamma), "beta": np.asarray(L0_xattn_ln_beta),
        "rs": np.asarray(L0_xattn_residual_scale).reshape(1),
        "router": rows_by_block(L0_ffn_router_gate), "gate_up": gu_l,
        "down": np.asarray(L0_ffn_expert_down).transpose(1, 0, 2),
    }
    arrays = {f"{k}_dram": np.ascontiguousarray(a) for k, a in arrays.items()}
    nc = bacc.Bacc("TRN2", target_bir_lowering=False, num_devices=1)
    args = [nc.dram_tensor(k, a.shape, mybir.dt.from_np(a.dtype), kind="ExternalInput").ap() for k, a in arrays.items()]
    args.append(nc.dram_tensor("out_dram", (ROWS, H), F32, kind="ExternalOutput").ap())
    flamingo(nc, *args)
    result = run_bass_kernel_spmd(nc, [arrays], core_ids=[0])
    return result.results[0]["out_dram"].reshape(B, S, H)
```
